# Optimizing a Trainium2 kernel written in Bass

```python
import numpy as np
import jax
import jax.numpy as jnp

def _softmax(x, axis=-1):
    return jax.nn.softmax(x, axis=axis)

def _gelu(x):
    return jax.nn.gelu(x, approximate=True)

def _silu(x):
    return jax.nn.silu(x)

def _sigmoid(x):
    return jax.nn.sigmoid(x)

def _layernorm(x, axis=-1, eps=1e-05):
    m = jnp.mean(x, axis=axis, keepdims=True)
    v = jnp.var(x, axis=axis, keepdims=True)
    return (x - m) / jnp.sqrt(v + eps)

def _scatter_add(tgt, idx, src, axis=0):
    return tgt.at[idx].add(src)

def _segment_sum(src, seg, n):
    return jax.ops.segment_sum(src, seg, n)
kernel_name = 'mk_adaln_d1_jaxref_r4_9dfe2f'

def setup_inputs(seed: int=0):
    np.random.seed(seed)
    _w = jnp.asarray

    def _L0_attn_setup():
        import jax, jax.numpy as jnp
        import numpy as np
        import math
        B, L, H = (2, 512, 512)
        NH, HD, RD = (16, 128, 64)
        QR, KVR = (192, 128)

        def rotate_half(x):
            d = x.shape[-1]
            x1, x2 = (x[..., :d // 2], x[..., d // 2:])
            return jnp.concatenate([-x2, x1], axis=-1)

        def apply_rope(x):
            d = x.shape[-1]
            seq_len = x.shape[1]
            inv_freq = 1.0 / 10000.0 ** (jnp.arange(0, d, 2, dtype=x.dtype) / d)
            pos = jnp.arange(seq_len, dtype=x.dtype)
            freqs = jnp.outer(pos, inv_freq)
            cos = jnp.concatenate([jnp.cos(freqs), jnp.cos(freqs)], axis=-1)
            sin = jnp.concatenate([jnp.sin(freqs), jnp.sin(freqs)], axis=-1)
            if x.ndim == 4:
                cos, sin = (cos[None, :, None, :], sin[None, :, None, :])
            else:
                cos, sin = (cos[None, :, :], sin[None, :, :])
            return x * cos + rotate_half(x) * sin
        key = jax.random.key(seed)
        ks = jax.random.split(key, 9)
        sc = lambda fan_in: 1.0 / math.sqrt(fan_in)
        return {'x': jax.random.normal(ks[0], (B, L, H), jnp.float32), 'wq_down': jax.random.normal(ks[1], (H, QR), jnp.float32) * sc(H), 'wq_up': jax.random.normal(ks[2], (QR, NH * HD), jnp.float32) * sc(QR), 'wq_rope': jax.random.normal(ks[3], (QR, NH * RD), jnp.float32) * sc(QR), 'wkv_down': jax.random.normal(ks[4], (H, KVR), jnp.float32) * sc(H), 'wk_up': jax.random.normal(ks[5], (KVR, NH * HD), jnp.float32) * sc(KVR), 'wv_up': jax.random.normal(ks[6], (KVR, NH * HD), jnp.float32) * sc(KVR), 'wk_rope': jax.random.normal(ks[7], (H, RD), jnp.float32) * sc(H), 'wo': jax.random.normal(ks[8], (NH * HD, H), jnp.float32) * sc(NH * HD)}
    _L0_attn_in = _L0_attn_setup()

    def _L0_ffn_setup():
        import jax, jax.numpy as jnp
        import numpy as np
        B, S, H = (2, 512, 512)
        E, K = (16, 4)
        I_MOE, I_SH = (352, 1408)
        key = jax.random.key(seed)
        ks = jax.random.split(key, 9)

        def w(k, shape, fan_in):
            return jax.random.normal(k, shape, jnp.float32) * fan_in ** (-0.5)
        return {'hidden_states': jax.random.normal(ks[0], (B, S, H), jnp.float32), 'router_w': w(ks[1], (E, H), H), 'w_gate': w(ks[2], (E, H, I_MOE), H), 'w_up': w(ks[3], (E, H, I_MOE), H), 'w_down': w(ks[4], (E, I_MOE, H), I_MOE), 'sh_gate': w(ks[5], (H, I_SH), H), 'sh_up': w(ks[6], (H, I_SH), H), 'sh_down': w(ks[7], (I_SH, H), I_SH), 'sh_gate_w': w(ks[8], (H, 1), H)}
    _L0_ffn_in = _L0_ffn_setup()
    _L0_c = _w((lambda *s: np.random.randn(*s).astype(np.float32) * 0.05)(4, 512))
    _L0_wmod = _w((lambda *s: np.random.randn(*s).astype(np.float32) * 0.05)(512, 6 * 512) * 512 ** (-0.5))
    _d = {'L0_attn_x': _L0_attn_in['x'], 'L0_attn_wq_down': _L0_attn_in['wq_down'], 'L0_attn_wq_up': _L0_attn_in['wq_up'], 'L0_attn_wq_rope': _L0_attn_in['wq_rope'], 'L0_attn_wkv_down': _L0_attn_in['wkv_down'], 'L0_attn_wk_up': _L0_attn_in['wk_up'], 'L0_attn_wv_up': _L0_attn_in['wv_up'], 'L0_attn_wk_rope': _L0_attn_in['wk_rope'], 'L0_attn_wo': _L0_attn_in['wo'], 'L0_ffn_router_w': _L0_ffn_in['router_w'], 'L0_ffn_w_gate': _L0_ffn_in['w_gate'], 'L0_ffn_w_up': _L0_ffn_in['w_up'], 'L0_ffn_w_down': _L0_ffn_in['w_down'], 'L0_ffn_sh_gate': _L0_ffn_in['sh_gate'], 'L0_ffn_sh_up': _L0_ffn_in['sh_up'], 'L0_ffn_sh_down': _L0_ffn_in['sh_down'], 'L0_ffn_sh_gate_w': _L0_ffn_in['sh_gate_w'], 'L0_c': _L0_c, 'L0_wmod': _L0_wmod}
    _x0 = _d['L0_attn_x']
    _d['L0_attn_x'] = jax.random.normal(jax.random.fold_in(jax.random.key(seed), 1), (4, 512, 512), dtype=_x0.dtype)
    del _x0
    return _d

def reference(L0_attn_x, L0_attn_wq_down, L0_attn_wq_up, L0_attn_wq_rope, L0_attn_wkv_down, L0_attn_wk_up, L0_attn_wv_up, L0_attn_wk_rope, L0_attn_wo, L0_ffn_router_w, L0_ffn_w_gate, L0_ffn_w_up, L0_ffn_w_down, L0_ffn_sh_gate, L0_ffn_sh_up, L0_ffn_sh_down, L0_ffn_sh_gate_w, L0_c, L0_wmod):

    def _L0_attn_ref(x, wq_down, wq_up, wq_rope, wkv_down, wk_up, wv_up, wk_rope, wo):
        import jax, jax.numpy as jnp
        import numpy as np
        import math
        B, L, H = (2, 512, 512)
        NH, HD, RD = (16, 128, 64)
        QR, KVR = (192, 128)

        def rotate_half(x):
            d = x.shape[-1]
            x1, x2 = (x[..., :d // 2], x[..., d // 2:])
            return jnp.concatenate([-x2, x1], axis=-1)

        def apply_rope(x):
            d = x.shape[-1]
            seq_len = x.shape[1]
            inv_freq = 1.0 / 10000.0 ** (jnp.arange(0, d, 2, dtype=x.dtype) / d)
            pos = jnp.arange(seq_len, dtype=x.dtype)
            freqs = jnp.outer(pos, inv_freq)
            cos = jnp.concatenate([jnp.cos(freqs), jnp.cos(freqs)], axis=-1)
            sin = jnp.concatenate([jnp.sin(freqs), jnp.sin(freqs)], axis=-1)
            if x.ndim == 4:
                cos, sin = (cos[None, :, None, :], sin[None, :, None, :])
            else:
                cos, sin = (cos[None, :, :], sin[None, :, :])
            return x * cos + rotate_half(x) * sin
        b, l, _ = x.shape
        q_latent = x @ wq_down
        q_content = (q_latent @ wq_up).reshape(b, l, NH, HD)
        q_rope = (q_latent @ wq_rope).reshape(b, l, NH, RD)
        q_rope = apply_rope(q_rope)
        kv_latent = x @ wkv_down
        k_content = (kv_latent @ wk_up).reshape(b, l, NH, HD)
        v = (kv_latent @ wv_up).reshape(b, l, NH, HD)
        k_rope = apply_rope(x @ wk_rope)
        k_rope = jnp.broadcast_to(k_rope[:, :, None, :], (b, l, NH, RD))
        q = jnp.concatenate([q_content, q_rope], axis=-1)
        k = jnp.concatenate([k_content, k_rope], axis=-1)
        scale = 1.0 / math.sqrt(HD + RD)
        scores = jnp.einsum('bqhd,bkhd->bhqk', q, k) * scale
        causal_mask = jnp.triu(jnp.ones((l, l), dtype=bool), k=1)
        scores = jnp.where(causal_mask[None, None], -jnp.inf, scores)
        attn = jax.nn.softmax(scores, axis=-1)
        out = jnp.einsum('bhqk,bkhd->bqhd', attn, v).reshape(b, l, NH * HD)
        return out @ wo

    def _L0_ffn_ref(hidden_states, router_w, w_gate, w_up, w_down, sh_gate, sh_up, sh_down, sh_gate_w):
        import jax, jax.numpy as jnp
        import numpy as np
        B, S, H = (2, 512, 512)
        E, K = (16, 4)
        I_MOE, I_SH = (352, 1408)
        orig = hidden_states.shape
        h = hidden_states.reshape(-1, orig[-1])
        N = h.shape[0]
        logits = h @ router_w.T
        probs = jax.nn.softmax(logits.astype(jnp.float32), axis=-1)
        top_vals, top_idx = jax.lax.top_k(probs, K)
        top_vals = top_vals / jnp.maximum(top_vals.sum(-1, keepdims=True), 1e-09)
        top_vals = top_vals.astype(h.dtype)
        comb = jnp.zeros((N, E), h.dtype).at[jnp.arange(N)[:, None], top_idx].add(top_vals)
        g = jnp.einsum('nh,ehi->eni', h, w_gate)
        u = jnp.einsum('nh,ehi->eni', h, w_up)
        y = jnp.einsum('eni,eih->enh', jax.nn.silu(g) * u, w_down)
        routed = jnp.einsum('enh,ne->nh', y, comb)
        shared = jax.nn.silu(h @ sh_gate) * (h @ sh_up) @ sh_down
        sg = jax.nn.sigmoid(h @ sh_gate_w)
        return (routed + sg * shared).reshape(orig)
    x = L0_attn_x
    mod = (_silu(L0_c) @ L0_wmod).reshape(L0_c.shape[0], 6, 1, -1)
    sa, ca, ga, sb, cb, gb = (mod[:, 0], mod[:, 1], mod[:, 2], mod[:, 3], mod[:, 4], mod[:, 5])
    ga = (2 * (ga >= 0) - 1) * jnp.maximum(jnp.abs(ga), 0.25)
    gb = (2 * (gb >= 0) - 1) * jnp.maximum(jnp.abs(gb), 0.25)
    h = _layernorm(x, axis=-1) * (1 + ca) + sa
    x = x + ga * _L0_attn_ref(h, L0_attn_wq_down, L0_attn_wq_up, L0_attn_wq_rope, L0_attn_wkv_down, L0_attn_wk_up, L0_attn_wv_up, L0_attn_wk_rope, L0_attn_wo)
    h = _layernorm(x, axis=-1) * (1 + cb) + sb
    x = x + gb * _L0_ffn_ref(h, L0_ffn_router_w, L0_ffn_w_gate, L0_ffn_w_up, L0_ffn_w_down, L0_ffn_sh_gate, L0_ffn_sh_up, L0_ffn_sh_down, L0_ffn_sh_gate_w)
    return x

_drawn_inputs = setup_inputs


def setup_inputs(seed=0):
    import zlib

    import numpy as np

    out = dict(_drawn_inputs(seed))
    spreads = {}
    factors = {'L0_attn_wq_rope': 2.867, 'L0_attn_wk_rope': 2.846}
    for name, (base, spread) in spreads.items():
        noise = np.random.default_rng([zlib.crc32(name.encode()), seed]).standard_normal(out[name].shape)
        drawn = base * np.exp(spread * noise) if base else spread * noise
        out[name] = jnp.asarray(drawn.astype(out[name].dtype))
    for name, factor in factors.items():
        out[name] = (out[name] * factor).astype(out[name].dtype)
    return out
```

```python
from contextlib import ExitStack

import concourse.bass as bass
from concourse import mybir

F32 = mybir.dt.float32
F32R = mybir.dt.float32r
BF16 = mybir.dt.bfloat16
U32 = mybir.dt.uint32
ALU = mybir.AluOpType
ACT = mybir.ActivationFunctionType
AX = mybir.AxisListType

P = 128
B, L, H = 4, 512, 512
NH, HD, RD = 16, 128, 64
QR, KVR = 192, 128
E, TOPK, IM, ISH = 16, 4, 352, 1408
N = B * L
KC = H // P
TT = L // P
NT = N // P
QX = QR - P
SCALE = 1.0 / float(HD + RD) ** 0.5
EPS = 1e-5
MASKED = -1e30
NMOD = 6
HG = 4
NG = NH // HG
SLOTS = 6
DOWN = 5 * P
NS = ISH // IM
RW = E + 1
IC = [(0, 128), (128, 128), (256, 96)]
WIDTH = [max(256, (i + 1) * P) for i in range(TT)]


def r32(ap):
    return ap.bitcast(F32)


def hold(eng, sem, value, passed):
    eng.wait_ge(sem, value)
    eng.sem_inc(passed, 1)


def setup_block(nc, t, d):
    with ExitStack() as ctx:
        def sb(name, shape, dt=F32):
            return ctx.enter_context(nc.sbuf_tensor(name, shape, dt))

        def sem(name):
            return ctx.enter_context(nc.semaphore(name))

        c_row = sb("c_row", [B, H])
        c_exp = sb("c_exp", [B, H])
        c_den = sb("c_den", [B, H])
        c_silu = sb("c_silu", [B, H])
        c_T = sb("c_T", [P, KC, B])
        wmod = sb("wmod", [P, 2, KC, H])
        gate_row = sb("gate_row", [B, H])
        gate_abs = sb("gate_abs", [B, H])
        gate_sgn = sb("gate_sgn", [B, H])
        gates = sb("gates", [B, 2, H])
        mask_f = sb("mask_f", [P, P])
        rw_row = sb("rw_row", [RW, H])
        down_raw = sb("down_raw", [P, KC, DOWN])
        wq_up = sb("wq_up", [P, NH * HD])
        wq_up1 = sb("wq_up1", [QX, NH * HD])
        wk_up = sb("wk_up", [P, NH * HD])
        wv_up = sb("wv_up", [P, NH * HD])
        wqr = sb("wqr", [P, NH * RD])
        wqr1 = sb("wqr1", [P, NH * RD])
        wo = sb("wo", [P, NH // 2, H])
        head_T = sb("head_T", [P, 2, 4 * P])
        head_w = sb("head_w", [P, 2, SLOTS, P], F32R)

        ps = ctx.enter_context(nc.psum_tensor("ps_setup", [P, 8, 512], F32))
        T_PS, M_PS, O_PS, C_PS, R_PS = (0, 1), (2, 3), (4, 5), 6, 7

        c_loaded = sem("c_loaded")
        consts_loaded = sem("consts_loaded")
        tables_loaded = sem("tables_loaded")
        down_loaded = sem("down_loaded")
        wmod_loaded = [sem(f"wmod_loaded{j}") for j in range(2)]
        up_loaded = [sem(f"up_loaded{half}") for half in range(2)]
        wo_loaded = [sem(f"wo_loaded{quarter}") for quarter in range(NG)]
        rope_loaded = sem("rope_loaded")
        router_loaded = sem("router_loaded")
        c_exp_ready = sem("c_exp_ready")
        c_step = sem("c_step")
        c_T_mm = sem("c_T_mm")
        c_T_ready = sem("c_T_ready")
        mod_mm = sem("mod_mm")
        mod_taken = sem("mod_taken")
        gate_step = sem("gate_step")
        gates_ready = sem("gates_ready")
        gates_stored = sem("gates_stored")
        router_mm = sem("router_mm")
        router_ready = sem("router_ready")
        down_hi = sem("down_hi")
        down_lo = sem("down_lo")
        mask_ready = sem("mask_ready")
        turned = sem("turned")
        turned_copied = sem("turned_copied")
        m_mm = sem("m_mm")
        o_mm = sem("o_mm")
        m_hi = sem("m_hi")
        m_lo = sem("m_lo")
        o_hi = sem("o_hi")
        o_lo = sem("o_lo")
        rope_hi = sem("rope_hi")
        rope_lo = sem("rope_lo")
        rope1_lo = sem("rope1_lo")
        head_stored = [sem(f"head_stored{par}") for par in range(2)]

        block = ctx.enter_context(nc.Block())

        def load_wo(sp, quarter):
            first = quarter * HG
            sp.dma_start(wo[:, first % (2 * HG):first % (2 * HG) + HG, :],
                         d["wo"].rearrange("(h p) n -> p h n", p=HD)[:, first:first + HG, :]).then_inc(
                wo_loaded[quarter], 16)

        @block.sync
        def _(sp):
            sp.dma_start(c_row[:, :], d["c"]).then_inc(c_loaded, 16)
            sp.dma_start(t["ident"][:, :], d["ident"]).then_inc(consts_loaded, 16)
            sp.dma_start(mask_f[:, :], d["mask"]).then_inc(consts_loaded, 16)
            for half in range(2):
                cols = slice(half * NH * HD // 2, (half + 1) * NH * HD // 2)
                sp.dma_start(wq_up[:, cols], d["wq_up"][0:P, cols]).then_inc(up_loaded[half], 16)
                sp.dma_start(wq_up1[:, cols], d["wq_up"][P:QR, cols]).then_inc(up_loaded[half], 16)
                sp.dma_start(wk_up[:, cols], d["wk_up"][:, cols]).then_inc(up_loaded[half], 16)
                sp.dma_start(wv_up[:, cols], d["wv_up"][:, cols]).then_inc(up_loaded[half], 16)
                load_wo(sp, half)
            for h in range(NH):
                sp.wait_ge(rope_lo, h + 1)
                sp.wait_ge(rope1_lo, 2 * h + 2)
                sp.wait_ge(m_lo, 2 * h + 2)
                sp.dma_start(r32(d["head_w"][h]), r32(head_w[:, h % 2, :, :].rearrange("p s c -> p (s c)"))).then_inc(
                    head_stored[h % 2], 16)
                if h in (HG - 1, 2 * HG - 1):
                    sp.wait_ge(o_mm, h + 1)
                    load_wo(sp, h // HG + 2)
            for par in range(2):
                sp.wait_ge(head_stored[par], 16 * NH // 2)

        @block.gpsimd
        def _(pool):
            for h in range(NH):
                cols = slice(h * RD, (h + 1) * RD)
                if h == 0:
                    pool.wait_ge(rope_loaded, 48)
                if h >= 2:
                    pool.wait_ge(head_stored[h % 2], 16 * (h // 2))
                for slot, raw in ((3, wqr), (5, wqr1)):
                    for half in range(2):
                        last = nc.gpsimd.tensor_copy(head_w[:, h % 2, slot, half * RD:(half + 1) * RD], raw[:, cols])
                last.then_inc(rope_hi, 1)
                pool.wait_ge(rope_hi, h + 1)
                for half in range(2):
                    out = slice(half * RD, (half + 1) * RD)
                    last = nc.gpsimd.tensor_tensor(head_w[:, h % 2, 4, out], wqr[:, cols],
                                                   r32(head_w[:, h % 2, 3, out]), ALU.subtract)
                last.then_inc(rope_lo, 1)

        @block.scalar
        def _(act):
            act.dma_start(wqr[:, :], d["wq_rope"][0:P, :]).then_inc(rope_loaded, 16)
            act.dma_start(wqr1[0:QX, :], d["wq_rope"][P:QR, :]).then_inc(rope_loaded, 16)
            act.dma_start(wqr1[QX:P, :], d["wq_rope"][P:QR, :]).then_inc(rope_loaded, 16)
            act.wait_ge(c_loaded, 16)
            nc.scalar.activation(c_exp[:, :], c_row[:, :], ACT.Exp, scale=-1.0).then_inc(c_exp_ready, 1)
            wmod_k = d["wmod"].rearrange("(k p) n -> p k n", p=P)
            for j in range(2):
                act.dma_start(wmod[:, j, :, :], wmod_k[:, :, j * H:(j + 1) * H]).then_inc(wmod_loaded[j], 16)
            wq, wkv, wkr = (d[k].rearrange("(k p) n -> p k n", p=P) for k in ("wq_down", "wkv_down", "wk_rope"))
            half = RD // 2
            pieces = [(0, wq, 0, QR), (QR, wq, P, QX), (2 * P, wkv, 0, KVR),
                      (3 * P, wkr, 0, RD), (3 * P + RD, wkr, half, half), (3 * P + RD + half, wkr, 0, half),
                      (4 * P, wkr, half, half), (4 * P + half, wkr, 0, half), (4 * P + RD, wkr, 0, RD)]
            for dst, src, at, width in pieces:
                act.dma_start(down_raw[:, :, dst:dst + width], src[:, :, at:at + width]).then_inc(down_loaded, 16)
            act.dma_start(rw_row[0:E, :], d["router_w"]).then_inc(router_loaded, 16)
            act.dma_start(rw_row[E:RW, :], d["sh_gate_w"].rearrange("n a -> a n")).then_inc(router_loaded, 16)
            for name in ("rope_q", "rope_kc", "rope_ks"):
                act.dma_start(t[name][:, :], d[name]).then_inc(tables_loaded, 16)
            for h in range(NH):
                act.wait_ge(m_mm, h + 1)
                if h >= 2:
                    act.wait_ge(head_stored[h % 2], 16 * (h // 2))
                nc.scalar.activation(head_w[:, h % 2, 0, :], ps[:, M_PS[h % 2], 0:P], ACT.Copy)
                nc.scalar.activation(head_w[:, h % 2, 2, :], ps[:, M_PS[h % 2], P:2 * P], ACT.Copy).then_inc(m_hi, 1)
                act.wait_ge(o_mm, h + 1)
                nc.scalar.activation(t["wo_hi"][:, h, :], ps[:, O_PS[h % 2], :], ACT.Copy).then_inc(o_hi, 1)
                if h < NMOD - 2:
                    act.wait_ge(mod_mm, h + 1)
                    act.dma_start(wmod[:, h % 2, :, :], wmod_k[:, :, (h + 2) * H:(h + 3) * H]).then_inc(
                        wmod_loaded[h % 2], 16)
            act.wait_ge(tables_loaded, 48)
            act.wait_ge(gates_ready, 2)
            act.dma_start(d["gates"], gates[:, :, :]).then_inc(gates_stored, 16)
            act.wait_ge(gates_stored, 16)

        def turn(pe, h):
            if h % (NH // 2) == 0:
                pe.wait_ge(up_loaded[h // (NH // 2)], 64)
            if h >= 2:
                pe.wait_ge(turned_copied, h - 1)
            cols = slice(h * HD, (h + 1) * HD)
            bank = T_PS[h % 2]
            ident = t["ident"]
            nc.tensor.transpose(ps[:, bank, 0:P], wq_up[:, cols], ident[:, :])
            nc.tensor.transpose(ps[:, bank, P:P + QX], wq_up1[:, cols], ident[0:QX, 0:QX])
            nc.tensor.transpose(ps[:, bank, P + QX:2 * P], wq_up1[:, cols], ident[0:QX, 0:QX])
            nc.tensor.transpose(ps[:, bank, 2 * P:3 * P], wk_up[:, cols], ident[:, :])
            nc.tensor.transpose(ps[:, bank, 3 * P:4 * P], wv_up[:, cols], ident[:, :]).then_inc(turned, 1)

        @block.tensor
        def _(pe):
            pe.wait_ge(consts_loaded, 32)
            pe.wait_ge(c_step, 3)
            for k in range(KC):
                last = nc.tensor.transpose(ps[:, C_PS, k * B:(k + 1) * B], c_silu[:, k * P:(k + 1) * P],
                                           t["ident"][0:B, 0:B])
            last.then_inc(c_T_mm, 1)
            turn(pe, 0)
            for h in range(NH):
                if h + 1 < NH:
                    turn(pe, h + 1)
                pe.wait_ge(turned_copied, h + 1)
                if h >= 2:
                    pe.wait_ge(m_lo, 2 * (h - 1))
                    pe.wait_ge(o_lo, h - 1)
                T = head_T[:, h % 2, :]
                nc.tensor.matmul(ps[:, M_PS[h % 2], 0:P], T[:, 0:P], T[:, 2 * P:3 * P], start=True, stop=True)
                nc.tensor.matmul(ps[:, M_PS[h % 2], P:2 * P], T[:, P:2 * P], T[:, 2 * P:3 * P],
                                 start=True, stop=True).then_inc(m_mm, 1)
                if h % HG == 0:
                    pe.wait_ge(wo_loaded[h // HG], 16)
                nc.tensor.matmul(ps[:, O_PS[h % 2], :], T[:, 3 * P:4 * P], wo[:, h % (2 * HG), :],
                                 start=True, stop=True).then_inc(o_mm, 1)
                if h < NMOD:
                    if h == 0:
                        pe.wait_ge(c_T_ready, 1)
                    else:
                        pe.wait_ge(mod_taken, h)
                    pe.wait_ge(wmod_loaded[h % 2], 16 * (h // 2 + 1))
                    if h % 3 == 2:
                        for k in range(KC):
                            last = nc.tensor.matmul(ps[0:B, C_PS, :], c_T[:, k, :], wmod[:, h % 2, k, :],
                                                    start=(k == 0), stop=(k == KC - 1))
                    else:
                        for c in range(KC):
                            for k in range(KC):
                                last = nc.tensor.matmul(ps[:, C_PS, c * B:(c + 1) * B],
                                                        wmod[:, h % 2, k, c * P:(c + 1) * P], c_T[:, k, :],
                                                        start=(k == 0), stop=(k == KC - 1))
                    last.then_inc(mod_mm, 1)
                if h == NMOD:
                    pe.wait_ge(router_loaded, 32)
                    for k in range(KC):
                        last = nc.tensor.transpose(ps[:, R_PS, k * RW:(k + 1) * RW], rw_row[:, k * P:(k + 1) * P],
                                                   t["ident"][0:RW, 0:RW])
                    last.then_inc(router_mm, 1)

        def split_products(dve, h):
            dve.wait_ge(m_hi, h + 1)
            nc.vector.tensor_tensor(head_w[:, h % 2, 1, :], ps[:, M_PS[h % 2], 0:P], r32(head_w[:, h % 2, 0, :]),
                                    ALU.subtract).then_inc(m_lo, 1)
            nc.vector.tensor_tensor(head_w[QX:P, h % 2, 2, :], ps[QX:P, M_PS[h % 2], P:2 * P],
                                    r32(head_w[QX:P, h % 2, 2, :]), ALU.subtract).then_inc(m_lo, 1)
            dve.wait_ge(rope_hi, h + 1)
            for half in range(2):
                out = slice(half * RD, (half + 1) * RD)
                nc.vector.tensor_tensor(head_w[QX:P, h % 2, 5, out], wqr1[QX:P, h * RD:(h + 1) * RD],
                                        r32(head_w[QX:P, h % 2, 5, out]), ALU.subtract).then_inc(rope1_lo, 1)
            dve.wait_ge(o_hi, h + 1)
            nc.vector.tensor_tensor(t["wo_lo"][:, h, :], ps[:, O_PS[h % 2], :], r32(t["wo_hi"][:, h, :]),
                                    ALU.subtract).then_inc(o_lo, 1)

        def take_mod(dve, j):
            dve.wait_ge(mod_mm, j + 1)
            half, kind = j // 3, j % 3
            if kind < 2:
                out = t["mod"][:, :, (half * 2 + kind) * KC:(half * 2 + kind + 1) * KC]
                nc.vector.tensor_scalar_add(out, ps[:, C_PS, 0:KC * B].rearrange("p (k b) -> p b k", b=B),
                                            float(kind)).then_inc(mod_taken, 1)
                return
            nc.vector.tensor_copy(gate_row[:, :], ps[0:B, C_PS, :]).then_inc(mod_taken, 1)
            dve.wait_ge(mod_taken, j + 1)
            nc.vector.scalar_tensor_tensor(gate_abs[:, :], gate_row[:, :], -1.0, gate_row[:, :],
                                           ALU.mult, ALU.max).then_inc(gate_step, 1)
            nc.vector.tensor_scalar(gate_sgn[:, :], gate_row[:, :], 0.0, 2.0, ALU.is_ge,
                                    ALU.mult).then_inc(gate_step, 1)
            dve.wait_ge(gate_step, 3 * half + 2)
            nc.vector.tensor_scalar_max(gate_abs[:, :], gate_abs[:, :], 0.25).then_inc(gate_step, 1)
            dve.wait_ge(gate_step, 3 * half + 3)
            nc.vector.scalar_tensor_tensor(gates[:, half, :], gate_sgn[:, :], -1.0, gate_abs[:, :],
                                           ALU.add, ALU.mult).then_inc(gates_ready, 1)

        @block.vector
        def _(dve):
            nc.vector.memset(t["eps"][:, :], EPS)
            dve.wait_ge(c_exp_ready, 1)
            nc.vector.tensor_scalar_add(c_exp[:, :], c_exp[:, :], 1.0).then_inc(c_step, 1)
            dve.wait_ge(c_step, 1)
            nc.vector.reciprocal(c_den[:, :], c_exp[:, :]).then_inc(c_step, 1)
            dve.wait_ge(c_step, 2)
            nc.vector.tensor_tensor(c_silu[:, :], c_row[:, :], c_den[:, :], ALU.mult).then_inc(c_step, 1)
            dve.wait_ge(consts_loaded, 32)
            nc.vector.tensor_copy(t["mask"][:, :], mask_f[:, :]).then_inc(mask_ready, 1)
            nc.vector.tensor_copy(t["ident_b"][:, :], t["ident"][:, :]).then_inc(mask_ready, 1)
            dve.wait_ge(c_T_mm, 1)
            nc.vector.tensor_copy(c_T[:, :, :].rearrange("p k b -> p (k b)"), ps[:, C_PS, 0:KC * B]).then_inc(
                c_T_ready, 1)
            for h in range(NH):
                dve.wait_ge(turned, h + 1)
                if h >= 2:
                    dve.wait_ge(o_mm, h - 1)
                nc.vector.tensor_copy(head_T[:, h % 2, :], ps[:, T_PS[h % 2], :]).then_inc(turned_copied, 1)
                if h >= 1:
                    split_products(dve, h - 1)
                if 1 <= h <= NMOD:
                    take_mod(dve, h - 1)
                if h == NMOD + 1:
                    dve.wait_ge(router_mm, 1)
                    nc.vector.tensor_copy(t["router_T"][:, :, :].rearrange("p k e -> p (k e)"),
                                          ps[:, R_PS, 0:KC * RW]).then_inc(router_ready, 1)
                if h == 1:
                    dve.wait_ge(down_loaded, 16 * 9)
                if 1 <= h <= KC:
                    nc.vector.tensor_copy(t["down_hi"][:, h - 1, :], down_raw[:, h - 1, :]).then_inc(down_hi, 1)
                if 2 <= h <= KC + 1:
                    dve.wait_ge(down_hi, h - 1)
                    nc.vector.tensor_tensor(t["down_lo"][:, h - 2, :], down_raw[:, h - 2, :],
                                            r32(t["down_hi"][:, h - 2, :]), ALU.subtract).then_inc(down_lo, 1)
            split_products(dve, NH - 1)


def attention_block(nc, t, d):
    with ExitStack() as ctx:
        def sb(name, shape, dt=F32):
            return ctx.enter_context(nc.sbuf_tensor(name, shape, dt))

        def sem(name):
            return ctx.enter_context(nc.semaphore(name))

        xt = sb("xt", [P, TT, H])
        probs = sb("probs", [P, 2, TT, L])
        normed, full = probs[:, 1, :, :], probs[:, 0, :, :]
        ctx_hi = sb("ctx_hi", [P, HG, L], F32R)
        ctx_lo = sb("ctx_lo", [P, HG, L], F32R)
        h_hi, h_lo = ctx_hi, ctx_lo
        stats = sb("stats", [P, TT, 6])
        mv = sb("mv", [P, TT, 2])
        std = sb("std", [P, TT])
        rstd = sb("rstd", [P, TT])
        mod_b = sb("mod_b", [P, 4 * KC])
        ga_b = sb("ga_b", [P, H])
        q0_hi = sb("q0_hi", [P, L], F32R)
        q0_lo = sb("q0_lo", [P, L], F32R)
        q1_hi2 = sb("q1_hi2", [P, L], F32R)
        q1_lo = sb("q1_lo", [QX, L], F32R)
        kv_hi = sb("kv_hi", [P, L], F32R)
        kv_lo = sb("kv_lo", [P, L], F32R)
        kr_hi = sb("kr_hi", [P, L], F32R)
        kr_lo = sb("kr_lo", [P, L], F32R)
        v_hi = sb("v_hi", [P, TT, KVR], F32R)
        v_lo = sb("v_lo", [P, TT, KVR], F32R)
        head_w = sb("head_w_in", [P, 2, SLOTS, P], F32R)
        qc_hi = sb("qc_hi", [P, 2, L], F32R)
        qc_lo = sb("qc_lo", [P, 2, L], F32R)
        qr_full = sb("qr_full", [P, L])
        qr_hi = sb("qr_hi", [P, 2, L], F32R)
        qr_lo = sb("qr_lo", [P, 2, L], F32R)
        mx = sb("mx", [P, 2, TT])
        nmx = sb("nmx", [P, 2, TT])
        sums = sb("sums", [P, 2, TT])
        rsum = sb("rsum", [P, 2, TT])
        pt_hi = sb("pt_hi", [P, TT, L], F32R)
        pt_lo = sb("pt_lo", [P, TT, L], F32R)
        gated = sb("gated", [P, 2, H])

        ps = ctx.enter_context(nc.psum_tensor("ps_attn", [P, 8, 512], F32))
        QC, QRP, S0, PT, CT = 0, 1, 2, 6, 7
        PROJ = [0, 1, 6, 7, 2]

        x_loaded = sem("x_loaded")
        ga_loaded = sem("ga_loaded")
        head_loaded = [sem(f"head_loaded{par}") for par in range(2)]
        x1_stored = sem("x1_stored")
        h2_stored = sem("h2_stored")
        stats_ready = sem("stats_ready")
        mv_ready = sem("mv_ready")
        std_ready = sem("std_ready")
        rstd_ready = sem("rstd_ready")
        normed_ready = sem("normed_ready")
        normed_T = sem("normed_T")
        mod_ready = sem("mod_ready")
        full_ready = sem("full_ready")
        h_hi_ready = sem("h_hi_ready")
        h_lo_ready = sem("h_lo_ready")
        proj_mm = sem("proj_mm")
        lat_hi = sem("lat_hi")
        lat_lo = sem("lat_lo")
        kv_full_ready = sem("kv_full_ready")
        kr_parts = sem("kr_parts")
        kr_full_ready = sem("kr_full_ready")
        kr_lo_ready = sem("kr_lo_ready")
        v_T = sem("v_T")
        zeros_ready = sem("zeros_ready")
        passed = {name: sem(f"passed_{name}") for name in ("sp", "pool", "dve")}
        qr_mm = sem("qr_mm")
        qc_mm = sem("qc_mm")
        qr_full_ready = sem("qr_full_ready")
        qr_hi_ready = sem("qr_hi_ready")
        qr_lo_ready = sem("qr_lo_ready")
        qc_hi_ready = sem("qc_hi_ready")
        qc_lo_ready = sem("qc_lo_ready")
        scores_mm = sem("scores_mm")
        mx_ready = sem("mx_ready")
        nmx_ready = sem("nmx_ready")
        exp_done = sem("exp_done")
        rsum_ready = sem("rsum_ready")
        probs_ready = sem("probs_ready")
        probs_T = sem("probs_T")
        pt_hi_ready = sem("pt_hi_ready")
        pt_lo_ready = sem("pt_lo_ready")
        ctx_mm = sem("ctx_mm")
        ctx_hi_ready = sem("ctx_hi_ready")
        ctx_lo_ready = sem("ctx_lo_ready")
        out_mm = sem("out_mm")
        gated_ready = sem("gated_ready")
        x_added = sem("x_added")
        logits_mm = sem("logits_mm")
        logits_ready = sem("logits_ready")

        seeded = (x1_stored, normed_ready, gated_ready, qc_mm, h2_stored, qr_full_ready, qc_lo_ready, exp_done, pt_lo_ready, ctx_lo_ready, logits_ready, h_lo_ready, qr_lo_ready, ctx_mm, out_mm)
        with nc.Block() as seeds:
            @seeds.gpsimd
            def _(pool):
                for semaphore in seeded:
                    pool.sem_inc(semaphore, 1)

        def after(eng, semaphore, n):
            eng.wait_ge(semaphore, n + 1)

        block = ctx.enter_context(nc.Block())

        def steps(eng, b, step):
            step(b, 0, 0, first=True)
            with eng.Fori(0, NG - 1) as g:
                for j in range(1, HG + 1):
                    step(b, g * HG + j, j)
            for j in range(1, HG + 1):
                step(b, (NG - 1) * HG + j, j, last=(j >= HG - 1), tail=(j == HG))

        def at_head(b, k):
            return b * NH + k

        @block.sync
        def _(sp):
            with sp.Fori(0, B) as b:
                hold(sp, x1_stored, 1 + b * 16, passed["sp"])
                hold(sp, normed_ready, 1 + b * (2 * TT), passed["sp"])
                sp.dma_start(xt[:, :, :], d["x"][bass.ds(b, 1)].rearrange("a (t p) n -> p (a t) n", p=P)).then_inc(
                    x_loaded, 16)
                hold(sp, gated_ready, 1 + b * (NG * TT), passed["sp"])
                sp.dma_start(ga_b[:, :], d["gates"][bass.ds(b, 1), 0, :].to_broadcast([P, H])).then_inc(ga_loaded, 16)
                for h in range(2):
                    hold(sp, qc_mm, 1 + at_head(b, 0), passed["sp"])
                    sp.dma_start(r32(head_w[:, h, :, :].rearrange("p s c -> p (s c)")),
                                 r32(d["head_w"][h])).then_inc(head_loaded[h], 16)
                with sp.Fori(1, NH // 2) as pair:
                    for h in range(2):
                        hold(sp, qc_mm, 1 + at_head(b, pair * 2 + (h - 1)), passed["sp"])
                        sp.dma_start(r32(head_w[:, h, :, :].rearrange("p s c -> p (s c)")),
                                     r32(d["head_w"][bass.ds(pair * 2 + h, 1)].rearrange("a p s -> (a p) s"))
                                     ).then_inc(head_loaded[h], 16)
                hold(sp, x_added, b * (NG * TT) + NG * TT, passed["sp"])
                sp.dma_start(d["x1"][bass.ds(b, 1)].rearrange("a (t p) n -> p (a t) n", p=P),
                             xt[:, :, :]).then_inc(x1_stored, 16)
                for part, ready, name in ((h_hi, h_hi_ready, "h2_hi"), (h_lo, h_lo_ready, "h2_lo")):
                    hold(sp, ready, (ready is h_lo_ready) + b * (2 * KC) + 2 * KC, passed["sp"])
                    sp.dma_start(r32(d[name][:, :, bass.ds(b * L, L)].rearrange("c p n -> p c n")),
                                 r32(part[:, :, :])).then_inc(h2_stored, 16)
            after(sp, x1_stored, 16 * B)
            after(sp, h2_stored, 32 * B)

        @block.gpsimd
        def _(pool):
            nc.gpsimd.memset(r32(pt_hi[:, TT - 1, (TT - 2) * P:(TT - 1) * P]), 0.0).then_inc(zeros_ready, 1)
            nc.gpsimd.memset(r32(pt_lo[:, TT - 1, (TT - 2) * P:(TT - 1) * P]), 0.0).then_inc(zeros_ready, 1)

            def h_lows(r):
                for c in range(KC):
                    pool.wait_ge(h_hi_ready, r * KC + (c + 1))
                    nc.gpsimd.tensor_tensor(h_lo[:, c, :], full[:, c, :], r32(h_hi[:, c, :]),
                                            ALU.subtract).then_inc(h_lo_ready, 1)

            def rope_low(b, k, par):
                n = at_head(b, k)
                pool.wait_ge(qr_hi_ready, n + 1)
                nc.gpsimd.tensor_tensor(qr_lo[:, par, :], qr_full[:, :], r32(qr_hi[:, par, :]),
                                        ALU.subtract).then_inc(qr_lo_ready, 1)

            def step(b, k, j, first=False, last=False, tail=False):
                if not last:
                    rope_low(b, k + 1, (j + 1) % 2)
                if not tail:
                    par = j % 2
                    hold(pool, rsum_ready, at_head(b, k) + 1, passed["pool"])
                    for i in range(TT):
                        nc.gpsimd.tensor_scalar(probs[:, par, i, 0:(i + 1) * P], probs[:, par, i, 0:(i + 1) * P],
                                                rsum[:, par, i:i + 1], None, ALU.mult).then_inc(probs_ready, 1)
                if j == HG:
                    for tile in range(TT):
                        done = at_head(b, k) - HG + tile
                        after(pool, gated_ready, done + 1)
                        nc.gpsimd.tensor_tensor(xt[:, tile, :], xt[:, tile, :], gated[:, tile % 2, :],
                                                ALU.add).then_inc(x_added, 1)

            with pool.Fori(0, B) as b:
                after(pool, h2_stored, b * 32)
                h_lows(b * 2)
                pool.wait_ge(kr_parts, b * 2 + 2)
                nc.gpsimd.tensor_tensor(full[:, 3, :], full[:, 1, :], full[:, 2, :], ALU.add).then_inc(
                    kr_full_ready, 1)
                pool.wait_ge(lat_hi, b * 5 + 5)
                nc.gpsimd.tensor_tensor(kr_lo[:, :], full[:, 3, :], r32(kr_hi[:, :]), ALU.subtract).then_inc(
                    kr_lo_ready, 1)
                rope_low(b, 0, 0)
                steps(pool, b, step)
                h_lows(b * 2 + 1)

        @block.scalar
        def _(act):
            def norm(r):
                act.wait_ge(mv_ready, r * TT + TT)
                nc.scalar.activation(std[:, :], mv[:, :, 1], ACT.Sqrt, bias=t["eps"][:, :]).then_inc(std_ready, 1)
                for c in range(KC):
                    act.wait_ge(full_ready, r * KC + (c + 1))
                    nc.scalar.activation(h_hi[:, c, :], full[:, c, :], ACT.Copy).then_inc(h_hi_ready, 1)

            def query_high(b, k, par):
                after(act, qc_mm, at_head(b, k) + 1)
                nc.scalar.activation(qc_hi[:, par, :], ps[:, QC, :], ACT.Copy).then_inc(qc_hi_ready, 1)

            def probs_high(b, k, i):
                done = at_head(b, k) * TT
                act.wait_ge(probs_T, done + (i + 1))
                if i == 0:
                    after(act, ctx_mm, at_head(b, k))
                nc.scalar.activation(pt_hi[:, 0:i + 1, i * P:(i + 1) * P],
                                     ps[:, PT, 0:(i + 1) * P].rearrange("p (k q) -> p k q", q=P),
                                     ACT.Copy).then_inc(pt_hi_ready, 1)

            def exps(b, k, par, i):
                act.wait_ge(nmx_ready, at_head(b, k) * TT + (i + 1))
                nc.scalar.activation(probs[:, par, i, 0:(i + 1) * P], ps[:, S0 + i, 0:(i + 1) * P], ACT.Exp,
                                     bias=nmx[:, par, i:i + 1], scale=SCALE,
                                     accum_out=sums[:, par, i:i + 1]).then_inc(exp_done, 1)

            def step(b, k, j, first=False, last=False, tail=False):
                for i in range(TT):
                    if i == TT - 1 and not last:
                        query_high(b, k + 1, (j + 1) % 2)
                    if not first:
                        probs_high(b, k - 1, i)
                    if not tail:
                        exps(b, k, j % 2, i)
                if not first:
                    after(act, ctx_mm, at_head(b, k))
                    if j == 1:
                        after(act, out_mm, at_head(b, k) - 1)
                    nc.scalar.activation(ctx_hi[:, j - 1, :], ps[:, CT, :], ACT.Copy).then_inc(ctx_hi_ready, 1)

            with act.Fori(0, B) as b:
                after(act, h2_stored, b * 32)
                norm(b * 2)
                for m, (out, bank) in enumerate(((q0_hi[:, :], 0), (q1_hi2[:, :], 1), (kv_hi[:, :], 6))):
                    act.wait_ge(proj_mm, b * 5 + (m + 1))
                    nc.scalar.activation(out, ps[:, bank, :], ACT.Copy).then_inc(lat_hi, 1)
                act.wait_ge(v_T, b + 1)
                nc.scalar.activation(v_hi[:, :, :].rearrange("p t c -> p (t c)"), ps[:, 3, :], ACT.Copy).then_inc(
                    lat_hi, 1)
                act.wait_ge(kr_full_ready, b + 1)
                nc.scalar.activation(kr_hi[:, :], full[:, 3, :], ACT.Copy).then_inc(lat_hi, 1)
                query_high(b, 0, 0)
                steps(act, b, step)
                norm(b * 2 + 1)

        @block.tensor
        def _(pe):
            def turn_normed(r):
                after(pe, normed_ready, r * TT + TT)
                for c in range(KC):
                    for i in range(TT):
                        last = nc.tensor.transpose(ps[:, S0 + c, i * P:(i + 1) * P], normed[:, i, c * P:(c + 1) * P],
                                                   t["ident"][:, :])
                    last.then_inc(normed_T, 1)

            def three(out, w_hi, w_lo, x_hi, x_lo, start, stop):
                nc.tensor.matmul(out, w_hi, x_hi, start=start, stop=False)
                nc.tensor.matmul(out, w_hi, x_lo, start=False, stop=False)
                return nc.tensor.matmul(out, w_lo, x_hi, start=False, stop=stop)

            def queries(b, k, par):
                n = at_head(b, k)
                pe.wait_ge(head_loaded[par], n * 8 + (16 - 8 * par))
                for bank, slot, mm, free in ((QRP, 3, qr_mm, qr_full_ready), (QC, 0, qc_mm, qc_lo_ready)):
                    after(pe, free, n)
                    three(ps[:, bank, :], head_w[:, par, slot, :], head_w[:, par, slot + 1, :], q0_hi[:, :],
                          q0_lo[:, :], True, False)
                    nc.tensor.matmul(ps[:, bank, :], head_w[:, par, slot + 2, :], q1_hi2[:, :], start=False,
                                     stop=False)
                    nc.tensor.matmul(ps[:, bank, :], head_w[0:QX, par, slot + 2, :], q1_lo[:, :], start=False,
                                     stop=True).then_inc(mm, 1)

            def score(b, k, par, i, first):
                n = at_head(b, k)
                if i == 0:
                    after(pe, qc_lo_ready, n + 1)
                    after(pe, qr_lo_ready, n + 1)
                after(pe, exp_done, n * TT if first else n * TT + (i + 1 - TT))
                out = ps[:, S0 + i, 0:WIDTH[i]]
                q, keys = slice(i * P, (i + 1) * P), slice(0, WIDTH[i])
                three(out, qc_hi[:, par, q], qc_lo[:, par, q], kv_hi[:, keys], kv_lo[:, keys], True, False)
                nc.tensor.matmul(ps[:, S0 + i, i * P:(i + 1) * P], t["ident_b"][:, :], t["mask"][:, :], start=False,
                                 stop=False, skip_group_check=True)
                three(out, qr_hi[:, par, q], qr_lo[:, par, q], kr_hi[:, keys], kr_lo[:, keys], False,
                      True).then_inc(scores_mm, 1)

            def turn_probs(b, k, par, i, after_out=False):
                n = at_head(b, k)
                pe.wait_ge(probs_ready, n * TT + (i + 1))
                after(pe, pt_lo_ready, n * TT + i)
                if after_out:
                    after(pe, gated_ready, n)
                for c in range(i + 1):
                    last = nc.tensor.transpose(ps[:, PT, c * P:(c + 1) * P], probs[:, par, i, c * P:(c + 1) * P],
                                               t["ident"][:, :])
                last.then_inc(probs_T, 1)

            def context(b, k):
                n = at_head(b, k)
                after(pe, pt_lo_ready, n * TT + TT)
                after(pe, ctx_lo_ready, n)
                nc.tensor.matmul(ps[:, CT, :], v_hi[:, 0, :], pt_hi[:, 0, :], start=True, stop=False)
                nc.tensor.matmul(ps[:, CT, :], v_hi[:, 0, :], pt_lo[:, 0, :], start=False, stop=False)
                for c in range(1, TT):
                    first_q = min(c, TT - 2) * P
                    three(ps[:, CT, first_q:], v_hi[:, c, :], v_lo[:, c, :], pt_hi[:, c, first_q:],
                          pt_lo[:, c, first_q:], False, False)
                nc.tensor.matmul(ps[:, CT, :], v_lo[:, 0, :], pt_hi[:, 0, :], start=False,
                                 stop=True).then_inc(ctx_mm, 1)

            def project_out(b, k):
                n = at_head(b, k)
                after(pe, ctx_lo_ready, n)
                for tile in range(TT):
                    bank = PT + tile % 2
                    if tile >= 2:
                        after(pe, gated_ready, n - HG + (tile - 1))
                    for j in range(HG):
                        q = slice(tile * P, (tile + 1) * P)
                        head = bass.ds(k + (j - HG), 1) if not isinstance(k, int) else slice(k + j - HG, k + j - HG + 1)
                        w_hi, w_lo = (t[w][:, head, :].rearrange("p a n -> p (a n)") for w in ("wo_hi", "wo_lo"))
                        nc.tensor.matmul(ps[:, bank, :], ctx_hi[:, j, q], w_hi, start=(j == 0), stop=False)
                        nc.tensor.matmul(ps[:, bank, :], ctx_hi[:, j, q], w_lo, start=False, stop=False)
                        last = nc.tensor.matmul(ps[:, bank, :], ctx_lo[:, j, q], w_hi, start=False,
                                                stop=(j == HG - 1))
                    last.then_inc(out_mm, 1)

            def step(b, k, j, first=False, last=False, tail=False):
                for i in range(TT):
                    if i == TT - 1 and not last:
                        queries(b, k + 1, (j + 1) % 2)
                    if not first:
                        turn_probs(b, k - 1, (j - 1) % 2, i, after_out=(j == 1 and i == 0))
                    if not tail:
                        score(b, k, j % 2, i, first)
                if not first:
                    context(b, k - 1)
                if j == HG:
                    project_out(b, k)

            pe.wait_ge(zeros_ready, 2)
            with pe.Fori(0, B) as b:
                turn_normed(b * 2)
                after(pe, h_lo_ready, b * (2 * KC) + KC)
                after(pe, logits_ready, b)
                for m, bank in enumerate(PROJ):
                    cols = slice(m * P, (m + 1) * P)
                    for c in range(KC):
                        last = three(ps[:, bank, :], t["down_hi"][:, c, cols], t["down_lo"][:, c, cols],
                                     h_hi[:, c, :], h_lo[:, c, :], c == 0, c == KC - 1)
                    last.then_inc(proj_mm, 1)
                pe.wait_ge(kv_full_ready, b + 1)
                for i in range(TT):
                    last = nc.tensor.transpose(ps[:, 3, i * P:(i + 1) * P], full[:, 0, i * P:(i + 1) * P],
                                               t["ident"][:, :])
                last.then_inc(v_T, 1)
                pe.wait_ge(lat_lo, b * 4 + 2)
                queries(b, 0, 0)
                pe.wait_ge(lat_lo, b * 4 + 4)
                pe.wait_ge(kr_lo_ready, b + 1)
                steps(pe, b, step)
                turn_normed(b * 2 + 1)
                pe.wait_ge(full_ready, b * (2 * KC) + 2 * KC)
                after(pe, gated_ready, b * (NG * TT) + NG * TT)
                for i in range(TT):
                    for c in range(KC):
                        last = nc.tensor.matmul(ps[:, PT, i * RW:(i + 1) * RW], full[:, c, i * P:(i + 1) * P],
                                                t["router_T"][:, c, :], start=(c == 0), stop=(c == KC - 1))
                last.then_inc(logits_mm, 1)

        @block.vector
        def _(dve):
            def norm(r, which):
                for i in range(TT):
                    nc.vector.bn_stats(stats[:, i, :], xt[:, i, :]).then_inc(stats_ready, 1)
                for i in range(TT):
                    hold(dve, stats_ready, r * TT + (i + 1), passed["dve"])
                    nc.vector.bn_aggr(mv[:, i, :], stats[:, i, :]).then_inc(mv_ready, 1)
                dve.wait_ge(std_ready, r + 1)
                nc.vector.reciprocal(rstd[:, :], std[:, :]).then_inc(rstd_ready, 1)
                dve.wait_ge(rstd_ready, r + 1)
                dve.wait_ge(mv_ready, r * TT + TT)
                for i in range(TT):
                    nc.vector.tensor_scalar(normed[:, i, :], xt[:, i, :], mv[:, i, 0:1], rstd[:, i:i + 1],
                                            ALU.subtract, ALU.mult).then_inc(normed_ready, 1)
                after(dve, h_lo_ready, r * KC)
                for c in range(KC):
                    dve.wait_ge(normed_T, r * KC + (c + 1))
                    shift = mod_b[:, 2 * which * KC + c:2 * which * KC + c + 1]
                    scale = mod_b[:, (2 * which + 1) * KC + c:(2 * which + 1) * KC + c + 1]
                    nc.vector.tensor_scalar(full[:, c, :], ps[:, S0 + c, :], scale, shift, ALU.mult,
                                            ALU.add).then_inc(full_ready, 1)

            def low(out, bank, hi, ready):
                nc.vector.tensor_tensor(out, bank, r32(hi), ALU.subtract).then_inc(ready, 1)

            def query_rope(b, k, par):
                n = at_head(b, k)
                dve.wait_ge(qr_mm, n + 1)
                after(dve, qr_lo_ready, n)
                nc.vector.tensor_tensor(qr_full[:, :], ps[:, QRP, :], t["rope_q"][:, :], ALU.mult).then_inc(
                    qr_full_ready, 1)
                after(dve, qr_full_ready, n + 1)
                nc.vector.tensor_copy(qr_hi[:, par, :], qr_full[:, :]).then_inc(qr_hi_ready, 1)
                dve.wait_ge(qc_hi_ready, n + 1)
                low(qc_lo[:, par, :], ps[:, QC, :], qc_hi[:, par, :], qc_lo_ready)

            def probs_low(b, k, i):
                dve.wait_ge(pt_hi_ready, at_head(b, k) * TT + (i + 1))
                out = (slice(None), slice(0, i + 1), slice(i * P, (i + 1) * P))
                low(pt_lo[out], ps[:, PT, 0:(i + 1) * P].rearrange("p (k q) -> p k q", q=P), pt_hi[out],
                    pt_lo_ready)

            def maxima(b, k, par, i):
                done = at_head(b, k) * TT
                dve.wait_ge(scores_mm, done + (i + 1))
                nc.vector.reduce_max(mx[:, par, i:i + 1], ps[:, S0 + i, 0:(i + 1) * P], AX.X).then_inc(mx_ready, 1)
                dve.wait_ge(mx_ready, done + (i + 1))
                nc.vector.tensor_scalar(nmx[:, par, i:i + 1], mx[:, par, i:i + 1], -SCALE, None,
                                        ALU.mult).then_inc(nmx_ready, 1)

            def step(b, k, j, first=False, last=False, tail=False):
                for i in range(TT):
                    if i == TT - 1 and not last:
                        query_rope(b, k + 1, (j + 1) % 2)
                    if not first:
                        probs_low(b, k - 1, i)
                    if not tail:
                        maxima(b, k, j % 2, i)
                if not tail:
                    after(dve, exp_done, at_head(b, k) * TT + TT)
                    nc.vector.reciprocal(rsum[:, j % 2, :], sums[:, j % 2, :]).then_inc(rsum_ready, 1)
                if not first:
                    dve.wait_ge(ctx_hi_ready, at_head(b, k))
                    low(ctx_lo[:, j - 1, :], ps[:, CT, :], ctx_hi[:, j - 1, :], ctx_lo_ready)
                if j == HG:
                    for tile in range(TT):
                        done = at_head(b, k) - HG + tile
                        after(dve, out_mm, done + 1)
                        if tile >= 2:
                            dve.wait_ge(x_added, done - 1)
                        nc.vector.tensor_tensor(gated[:, tile % 2, :], ps[:, PT + tile % 2, :], ga_b[:, :],
                                                ALU.mult).then_inc(gated_ready, 1)

            with dve.Fori(0, B) as b:
                nc.vector.tensor_copy(mod_b[:, :], t["mod"][:, bass.ds(b, 1), :].rearrange("p a k -> p (a k)")
                                      ).then_inc(mod_ready, 1)
                dve.wait_ge(mod_ready, b + 1)
                dve.wait_ge(x_loaded, b * 16 + 16)
                norm(b * 2, 0)
                dve.wait_ge(lat_hi, b * 5 + 1)
                low(q0_lo[:, :], ps[:, 0, :], q0_hi[:, :], lat_lo)
                dve.wait_ge(lat_hi, b * 5 + 2)
                low(q1_lo[:, :], ps[0:QX, 1, :], q1_hi2[0:QX, :], lat_lo)
                dve.wait_ge(lat_hi, b * 5 + 3)
                nc.vector.tensor_copy(full[:, 0, :], ps[:, 6, :]).then_inc(kv_full_ready, 1)
                low(kv_lo[:, :], ps[:, 6, :], kv_hi[:, :], lat_lo)
                dve.wait_ge(proj_mm, b * 5 + 5)
                nc.vector.tensor_tensor(full[:, 1, :], ps[:, 7, :], t["rope_kc"][:, :], ALU.mult).then_inc(kr_parts, 1)
                nc.vector.tensor_tensor(full[:, 2, :], ps[:, 2, :], t["rope_ks"][:, :], ALU.mult).then_inc(kr_parts, 1)
                dve.wait_ge(lat_hi, b * 5 + 4)
                low(v_lo[:, :, :].rearrange("p t c -> p (t c)"), ps[:, 3, :], v_hi[:, :, :].rearrange("p t c -> p (t c)"),
                    lat_lo)
                dve.wait_ge(ga_loaded, b * 16 + 16)
                query_rope(b, 0, 0)
                steps(dve, b, step)
                dve.wait_ge(x_added, b * (NG * TT) + NG * TT)
                norm(b * 2 + 1, 1)
                dve.wait_ge(logits_mm, b + 1)
                nc.vector.tensor_copy(t["logits"][:, bass.ds(b * TT, TT), :].rearrange("p t e -> p (t e)"),
                                      ps[:, PT, 0:TT * RW]).then_inc(logits_ready, 1)


def block_kernel(nc, d):
    with ExitStack() as outer:
        def sb(name, shape, dt=F32):
            return outer.enter_context(nc.sbuf_tensor(name, shape, dt))

        t = {"logits": sb("logits", [P, NT, RW])}
        with ExitStack() as attn:
            def sa(name, shape, dt=F32):
                t[name] = attn.enter_context(nc.sbuf_tensor(name, shape, dt))

            sa("ident", [P, P])
            sa("ident_b", [P, P], BF16)
            sa("mask", [P, P], BF16)
            sa("eps", [P, 1])
            sa("rope_q", [P, L])
            sa("rope_kc", [P, L])
            sa("rope_ks", [P, L])
            sa("mod", [P, B, 4 * KC])
            sa("router_T", [P, KC, RW])
            sa("down_hi", [P, KC, DOWN], F32R)
            sa("down_lo", [P, KC, DOWN], F32R)
            sa("wo_hi", [P, NH, H], F32R)
            sa("wo_lo", [P, NH, H], F32R)
            setup_block(nc, t, d)
            attention_block(nc, t, d)
        moe_block(nc, t, d)


def shape_constants():
    import numpy as np
    inv_freq = (1.0 / np.float32(10000.0) ** (np.arange(0, RD, 2, dtype=np.float32) / np.float32(RD))).astype(np.float32)
    freqs = np.outer(np.arange(L, dtype=np.float32), inv_freq).astype(np.float32).T
    cos, sin = np.cos(freqs), np.sin(freqs)
    return {
        "ident": np.eye(P, dtype=np.float32),
        "expert_ids": np.tile(np.arange(E, dtype=np.float32), (P, 1)),
        "mask": np.triu(np.full((P, P), MASKED, np.float32), 1),
        "rope_q": np.concatenate([cos, cos, sin, sin]),
        "rope_kc": np.concatenate([cos, cos, cos, -cos]),
        "rope_ks": np.concatenate([-sin, sin, sin, sin]),
    }


SLICES = E + NS
GU = KC * 2 * IM


def route_block(nc, t, d):
    with ExitStack() as ctx:
        def sb(name, shape, dt=F32):
            return ctx.enter_context(nc.sbuf_tensor(name, shape, dt))

        def sem(name):
            return ctx.enter_context(nc.semaphore(name))

        expert_ids = sb("expert_ids", [P, E])
        top_logit = sb("top_logit", [P, NT])
        probs = sb("router_probs", [P, NT, E])
        psum_ = sb("prob_sum", [P, NT])
        pinv = sb("prob_inv", [P, NT])
        top = sb("top", [P, NT, 8])
        top_at = sb("top_at", [P, NT, 8], U32)
        top_id = sb("top_id", [P, NT, TOPK])
        chosen = sb("chosen", [P, TOPK, NT, E])
        gate_exp = sb("gate_exp", [P, NT])

        ids_loaded = sem("ids_loaded")
        shifted_ready = sem("shifted_ready")
        exp_ready = sem("exp_ready")
        gate_exp_ready = sem("gate_exp_ready")
        step_done = sem("step_done")
        block = ctx.enter_context(nc.Block())

        @block.sync
        def _(sp):
            sp.dma_start(expert_ids[:, :], d["expert_ids"]).then_inc(ids_loaded, 16)

        @block.scalar
        def _(act):
            nc.scalar.activation(gate_exp[:, :], t["logits"][:, :, E], ACT.Exp, scale=-1.0).then_inc(gate_exp_ready, 1)
            act.wait_ge(shifted_ready, 1)
            nc.scalar.activation(probs[:, :, :], probs[:, :, :], ACT.Exp).then_inc(exp_ready, 1)

        @block.vector
        def _(dve):
            done = [0]

            def step(ins):
                done[0] += 1
                ins.then_inc(step_done, 1)
                dve.wait_ge(step_done, done[0])

            def wide(ap, n=E):
                return ap.unsqueeze(2).to_broadcast([P, NT, n])

            logits = t["logits"][:, :, 0:E]
            step(nc.vector.tensor_reduce(top_logit[:, :], logits, AX.X, ALU.max))
            nc.vector.tensor_tensor(probs[:, :, :], logits, wide(top_logit[:, :]), ALU.subtract).then_inc(
                shifted_ready, 1)
            dve.wait_ge(gate_exp_ready, 1)
            step(nc.vector.tensor_scalar_add(gate_exp[:, :], gate_exp[:, :], 1.0))
            step(nc.vector.reciprocal(gate_exp[:, :], gate_exp[:, :]))
            for s in range(NS):
                step(nc.vector.tensor_copy(t["weight"][:, E + s, :], gate_exp[:, :]))
            dve.wait_ge(exp_ready, 1)
            step(nc.vector.tensor_reduce(psum_[:, :], probs[:, :, :], AX.X, ALU.add))
            step(nc.vector.reciprocal(pinv[:, :], psum_[:, :]))
            step(nc.vector.tensor_tensor(probs[:, :, :], probs[:, :, :], wide(pinv[:, :]), ALU.mult))
            for i in range(NT):
                last = nc.vector.max(top[:, i, :], probs[:, i, :])
            step(last)
            for i in range(NT):
                last = nc.vector.max_index(top_at[:, i, :], top[:, i, :], probs[:, i, :])
            step(last)
            step(nc.vector.tensor_copy(top_id[:, :, :], top_at[:, :, 0:TOPK]))
            step(nc.vector.tensor_reduce(psum_[:, :], top[:, :, 0:TOPK], AX.X, ALU.add))
            step(nc.vector.tensor_scalar_max(psum_[:, :], psum_[:, :], 1e-9))
            step(nc.vector.reciprocal(pinv[:, :], psum_[:, :]))
            step(nc.vector.tensor_tensor(top[:, :, 0:TOPK], top[:, :, 0:TOPK], wide(pinv[:, :], TOPK), ALU.mult))
            dve.wait_ge(ids_loaded, 16)
            ids = expert_ids[:, :].unsqueeze(1).to_broadcast([P, NT, E])
            for k in range(TOPK):
                step(nc.vector.tensor_tensor(chosen[:, k, :, :], ids, top_id[:, :, k:k + 1].to_broadcast([P, NT, E]),
                                             ALU.is_equal))
                step(nc.vector.tensor_tensor(chosen[:, k, :, :], chosen[:, k, :, :],
                                             top[:, :, k:k + 1].to_broadcast([P, NT, E]), ALU.mult))
                if k > 0:
                    step(nc.vector.tensor_tensor(chosen[:, 0, :, :], chosen[:, 0, :, :], chosen[:, k, :, :], ALU.add))
            nc.vector.tensor_copy(t["weight"][:, 0:E, :].rearrange("p e t -> p t e"), chosen[:, 0, :, :])


def experts_block(nc, t, d):
    with ExitStack() as ctx:
        def sb(name, shape, dt=F32):
            return ctx.enter_context(nc.sbuf_tensor(name, shape, dt))

        def sem(name):
            return ctx.enter_context(nc.semaphore(name))

        acc = t["acc"]
        h_hi = sb("h2_hi", [P, KC, N], F32R)
        h_lo = sb("h2_lo", [P, KC, N], F32R)
        gu_raw = sb("gu_raw", [P, KC, 2, IM])
        dn_raw = sb("dn_raw", [P, len(IC), H])
        gu_hi = sb("gu_hi", [P, 2, KC, 2 * IM], F32R)
        gu_lo = sb("gu_lo", [P, 2, KC, 2 * IM], F32R)
        dn_hi = sb("dn_hi", [P, 2, len(IC), H], F32R)
        dn_lo = sb("dn_lo", [P, 2, len(IC), H], F32R)
        silu = sb("silu", [P, 2, L])
        act_full = sb("act_full", [P, 2, L])
        act_hi = sb("act_hi", [P, len(IC), L], F32R)
        act_lo = sb("act_lo", [P, len(IC), L], F32R)
        weight_s = sb("weight_s", [P, 2, NT])
        ps = ctx.enter_context(nc.psum_tensor("ps_moe", [P, 8, 512], F32))
        Y = 4

        h_loaded = sem("h_loaded")
        w_loaded = sem("w_loaded")
        w_hi_ready = sem("w_hi_ready")
        w_lo_ready = sem("w_lo_ready")
        pads_ready = sem("pads_ready")
        up_mm = sem("up_mm")
        silu_ready = sem("silu_ready")
        act_full_ready = sem("act_full_ready")
        act_hi_ready = sem("act_hi_ready")
        act_lo_ready = sem("act_lo_ready")
        down_mm = sem("down_mm")
        y_added = sem("y_added")
        acc_zero = sem("acc_zero")
        weight_ready = sem("weight_ready")
        passed = {name: sem(f"passed_{name}") for name in ("sp", "pool", "dve")}

        seeded = (w_lo_ready, down_mm, y_added, act_full_ready, act_lo_ready)
        with nc.Block() as seeds:
            @seeds.gpsimd
            def _(pool):
                for semaphore in seeded:
                    pool.sem_inc(semaphore, 1)

        def after(eng, semaphore, n):
            eng.wait_ge(semaphore, n + 1)

        block = ctx.enter_context(nc.Block())
        NI = len(IC)

        def slices(eng, body):
            with eng.Fori(0, SLICES // 2) as pair:
                for par in range(2):
                    body(pair * 2 + par, par)

        @block.sync
        def _(sp):
            for part, name in ((h_hi, "h2_hi"), (h_lo, "h2_lo")):
                for b in range(B):
                    cols = slice(b * L, (b + 1) * L)
                    sp.dma_start(r32(part[:, :, cols]), r32(d[name][:, :, cols].rearrange("c p n -> p c n"))).then_inc(
                        h_loaded, 16)

            def load(s, gate, up, down):
                hold(sp, w_lo_ready, 1 + s * 2, passed["sp"])
                sp.dma_start(gu_raw[:, :, 0, :], gate).then_inc(w_loaded, 16)
                sp.dma_start(gu_raw[:, :, 1, :], up).then_inc(w_loaded, 16)
                sp.dma_start(dn_raw[:, 0:2, :], down[0:2 * P].rearrange("(c p) n -> p c n", p=P)).then_inc(w_loaded, 16)
                sp.dma_start(dn_raw[0:IM - 2 * P, 2, :], down[2 * P:IM]).then_inc(w_loaded, 16)

            with sp.Fori(0, E) as e:
                one = bass.ds(e, 1)
                load(e, d["w_gate"][one].rearrange("a (c p) i -> p (a c) i", p=P),
                     d["w_up"][one].rearrange("a (c p) i -> p (a c) i", p=P),
                     d["w_down"][one].rearrange("a i n -> (a i) n"))
            with sp.Fori(0, NS) as s:
                cols = bass.ds(s * IM, IM)
                load(s + E, d["sh_gate"].rearrange("(c p) i -> p c i", p=P)[:, :, cols],
                     d["sh_up"].rearrange("(c p) i -> p c i", p=P)[:, :, cols], d["sh_down"][cols])

        @block.gpsimd
        def _(pool):
            def body(s, par):
                pool.wait_ge(w_hi_ready, s * 2 + 1)
                for c in range(KC):
                    last = nc.gpsimd.tensor_tensor(gu_lo[:, par, c, :], gu_raw[:, c, :, :].rearrange("p a i -> p (a i)"),
                                            r32(gu_hi[:, par, c, :]), ALU.subtract)
                last.then_inc(w_lo_ready, 1)
                pool.wait_ge(w_hi_ready, s * 2 + 2)
                nc.gpsimd.tensor_tensor(dn_lo[:, par, :, :], dn_raw[:, :, :], r32(dn_hi[:, par, :, :]),
                                        ALU.subtract).then_inc(w_lo_ready, 1)
                for tb in range(B):
                    for i, (_, rows) in enumerate(IC):
                        m = s * (B * NI) + (tb * NI + i)
                        pool.wait_ge(act_hi_ready, m + 1)
                        nc.gpsimd.tensor_tensor(act_lo[0:rows, i, :], act_full[0:rows, (tb * NI + i) % 2, :],
                                                r32(act_hi[0:rows, i, :]), ALU.subtract).then_inc(act_lo_ready, 1)

            nc.gpsimd.memset(dn_raw[IM - 2 * P:P, 2, :], 0.0).then_inc(pads_ready, 1)
            pool.wait_ge(pads_ready, 1)
            slices(pool, body)

        @block.scalar
        def _(act):
            def body(s, par):
                for tb in range(B):
                    for i, (_, rows) in enumerate(IC):
                        mm = tb * NI + i
                        m = s * (B * NI) + mm
                        act.wait_ge(up_mm, m + 1)
                        nc.scalar.activation(silu[0:rows, mm % 2, :], ps[0:rows, 2 * (mm % 2), :],
                                             ACT.Silu).then_inc(silu_ready, 1)
                        act.wait_ge(act_full_ready, m + 2)
                        if i == 0:
                            after(act, down_mm, s * (B * TT) + tb * TT)
                        nc.scalar.activation(act_hi[0:rows, i, :], act_full[0:rows, mm % 2, :],
                                             ACT.Copy).then_inc(act_hi_ready, 1)

            slices(act, body)

        @block.tensor
        def _(pe):
            def three(out, w_hi, w_lo, x_hi, x_lo, start, stop):
                nc.tensor.matmul(out, w_hi, x_hi, start=start, stop=False)
                nc.tensor.matmul(out, w_hi, x_lo, start=False, stop=False)
                return nc.tensor.matmul(out, w_lo, x_hi, start=False, stop=stop)

            def body(s, par):
                after(pe, w_lo_ready, s * 2 + 2)
                for tb in range(B):
                    cols = slice(tb * L, (tb + 1) * L)
                    for i, (at, rows) in enumerate(IC):
                        mm = tb * NI + i
                        pe.wait_ge(act_full_ready, s * (B * NI) + mm) if mm >= 2 else after(
                            pe, act_full_ready, s * (B * NI))
                        for half in range(2):
                            w = slice(half * IM + at, half * IM + at + rows)
                            for c in range(KC):
                                last = three(ps[0:rows, 2 * (mm % 2) + half, :], gu_hi[:, par, c, w],
                                             gu_lo[:, par, c, w], h_hi[:, c, cols], h_lo[:, c, cols], c == 0,
                                             c == KC - 1)
                        last.then_inc(up_mm, 1)
                    after(pe, act_lo_ready, s * (B * NI) + (tb + 1) * NI)
                    for i in range(TT):
                        after(pe, y_added, s * (B * TT) + tb * TT) if i == 0 else None
                        q = slice(i * P, (i + 1) * P)
                        for c, (_, rows) in enumerate(IC):
                            last = three(ps[:, Y + i, :], act_hi[0:rows, c, q], act_lo[0:rows, c, q],
                                         dn_hi[0:rows, par, c, :], dn_lo[0:rows, par, c, :], c == 0, c == NI - 1)
                        last.then_inc(down_mm, 1)

            pe.wait_ge(h_loaded, 2 * B * 16)
            slices(pe, body)

        @block.vector
        def _(dve):
            def body(s, par):
                hold(dve, down_mm, 1 + (s - 1) * (B * TT) if par else 1 + s * (B * TT), passed["dve"])
                dve.wait_ge(w_loaded, s * 64 + 64)
                for c in range(KC):
                    last = nc.vector.tensor_copy(gu_hi[:, par, c, :], gu_raw[:, c, :, :].rearrange("p a i -> p (a i)"))
                last.then_inc(w_hi_ready, 1)
                nc.vector.tensor_copy(dn_hi[:, par, :, :], dn_raw[:, :, :]).then_inc(w_hi_ready, 1)
                nc.vector.tensor_copy(weight_s[:, par, :], t["weight"][:, bass.ds(s, 1), :].rearrange("p a t -> p (a t)")
                                      ).then_inc(weight_ready, 1)
                for tb in range(B):
                    for i, (_, rows) in enumerate(IC):
                        mm = tb * NI + i
                        m = s * (B * NI) + mm
                        dve.wait_ge(silu_ready, m + 1)
                        if mm >= 2:
                            after(dve, act_lo_ready, m - 1)
                        else:
                            after(dve, act_lo_ready, s * (B * NI))
                        nc.vector.tensor_tensor(act_full[0:rows, mm % 2, :], silu[0:rows, mm % 2, :],
                                                ps[0:rows, 2 * (mm % 2) + 1, :], ALU.mult).then_inc(act_full_ready, 1)
                    for i in range(TT):
                        tile = tb * TT + i
                        if tile == 0:
                            dve.wait_ge(weight_ready, s + 1)
                        dve.wait_ge(down_mm, s * (B * TT) + tile + 2)
                        nc.vector.scalar_tensor_tensor(acc[:, tile, :], ps[:, Y + i, :],
                                                       weight_s[:, par, tile:tile + 1], acc[:, tile, :],
                                                       ALU.mult, ALU.add).then_inc(y_added, 1)

            nc.vector.memset(acc[:, :, :], 0.0).then_inc(acc_zero, 1)
            dve.wait_ge(acc_zero, 1)
            dve.wait_ge(pads_ready, 1)
            slices(dve, body)


def finish_block(nc, t, d):
    with ExitStack() as ctx:
        x1 = ctx.enter_context(nc.sbuf_tensor("x1_in", [P, B, TT, H], F32))
        gb = ctx.enter_context(nc.sbuf_tensor("gb", [P, B, H], F32))
        loaded = [ctx.enter_context(nc.semaphore(f"x1_loaded{b}")) for b in range(B)]
        gated = ctx.enter_context(nc.semaphore("acc_gated"))
        added = ctx.enter_context(nc.semaphore("x1_added"))
        stored = ctx.enter_context(nc.semaphore("out_stored"))
        acc = t["acc"]
        block = ctx.enter_context(nc.Block())

        def tokens(ap, b):
            return ap[b].rearrange("(t p) n -> p t n", p=P)

        @block.sync
        def _(sp):
            for b in range(B):
                sp.dma_start(gb[:, b, :], d["gates"][b:b + 1, 1, :].to_broadcast([P, H])).then_inc(loaded[b], 16)
                sp.dma_start(x1[:, b, :, :], tokens(d["x1"], b)).then_inc(loaded[b], 16)
            for b in range(B):
                sp.wait_ge(added, (b + 1) * TT)
                sp.dma_start(tokens(d["out"], b), x1[:, b, :, :]).then_inc(stored, 16)
            sp.wait_ge(stored, 16 * B)

        @block.vector
        def _(dve):
            for b in range(B):
                dve.wait_ge(loaded[b], 32)
                for i in range(TT):
                    nc.vector.tensor_tensor(acc[:, b * TT + i, :], acc[:, b * TT + i, :], gb[:, b, :],
                                            ALU.mult).then_inc(gated, 1)

        @block.gpsimd
        def _(pool):
            for b in range(B):
                for i in range(TT):
                    pool.wait_ge(gated, b * TT + i + 1)
                    nc.gpsimd.tensor_tensor(x1[:, b, i, :], x1[:, b, i, :], acc[:, b * TT + i, :],
                                            ALU.add).then_inc(added, 1)


def moe_block(nc, t, d):
    with ExitStack() as ctx:
        t["acc"] = ctx.enter_context(nc.sbuf_tensor("acc", [P, NT, H], F32))
        t["weight"] = ctx.enter_context(nc.sbuf_tensor("weight", [P, SLICES, NT], F32))
        route_block(nc, t, d)
        experts_block(nc, t, d)
        finish_block(nc, t, d)


SCRATCH = {
    "head_w": ((NH, P, SLOTS * P), F32R),
    "gates": ((B, 2, H), F32),
    "x1": ((B, L, H), F32),
    "h2_hi": ((KC, P, N), F32R),
    "h2_lo": ((KC, P, N), F32R),
}


_INPUTS = {
    "x": "L0_attn_x", "c": "L0_c", "wmod": "L0_wmod", "wq_down": "L0_attn_wq_down", "wq_up": "L0_attn_wq_up",
    "wq_rope": "L0_attn_wq_rope", "wkv_down": "L0_attn_wkv_down", "wk_up": "L0_attn_wk_up",
    "wv_up": "L0_attn_wv_up", "wk_rope": "L0_attn_wk_rope", "wo": "L0_attn_wo", "router_w": "L0_ffn_router_w",
    "w_gate": "L0_ffn_w_gate", "w_up": "L0_ffn_w_up", "w_down": "L0_ffn_w_down", "sh_gate": "L0_ffn_sh_gate",
    "sh_up": "L0_ffn_sh_up", "sh_down": "L0_ffn_sh_down", "sh_gate_w": "L0_ffn_sh_gate_w",
}


def kernel(**inputs):
    import numpy as np
    import concourse.bacc as bacc
    from concourse.bass_utils import run_bass_kernel_spmd

    nc = bacc.Bacc("TRN2", target_bir_lowering=False, num_devices=1)
    arrays = {name: np.ascontiguousarray(inputs[key]) for name, key in _INPUTS.items()}
    arrays.update(shape_constants())
    d = {name: nc.dram_tensor(f"in_{name}", a.shape, mybir.dt.from_np(a.dtype), kind="ExternalInput").ap()
         for name, a in arrays.items()}
    for name, (shape, dt) in SCRATCH.items():
        d[name] = nc.dram_tensor(f"scratch_{name}", shape, dt).ap()
    d["out"] = nc.dram_tensor("out", (B, L, H), F32, kind="ExternalOutput").ap()
    block_kernel(nc, d)
    result = run_bass_kernel_spmd(nc, [{f"in_{name}": a for name, a in arrays.items()}], core_ids=[0])
    return result.results[0]["out"]
```

```python
from contextlib import ExitStack

import concourse.bass as bass
from concourse import mybir

F32 = mybir.dt.float32
F32R = mybir.dt.float32r
BF16 = mybir.dt.bfloat16
U32 = mybir.dt.uint32
I32 = mybir.dt.int32
ALU = mybir.AluOpType
ACT = mybir.ActivationFunctionType
AX = mybir.AxisListType

P = 128
B, L, H = 4, 512, 512
NH, HD, RD = 16, 128, 64
QR, KVR = 192, 128
E, TOPK, IM, ISH = 16, 4, 352, 1408
N = B * L
KC = H // P
TT = L // P
NT = N // P
QX = QR - P
SCALE = 1.0 / float(HD + RD) ** 0.5
EPS = 1e-5
MASKED = -1e30
NMOD = 6
HG = 4
NG = NH // HG
SLOTS = 6
DOWN = 5 * P
NS = ISH // IM
RW = E + 1
TS = 256
TILES = N * TOPK // TS + E
CHUNKS = TILES * TS // P
IC = [(0, 128), (128, 128), (256, 96)]
NI = len(IC)
WIDTH = [max(256, (i + 1) * P) for i in range(TT)]


def r32(ap):
    return ap.bitcast(F32)


def three(nc, out, w_hi, w_lo, x_hi, x_lo, start, stop):
    nc.tensor.matmul(out, w_hi, x_hi, start=start, stop=False)
    nc.tensor.matmul(out, w_hi, x_lo, start=False, stop=False)
    return nc.tensor.matmul(out, w_lo, x_hi, start=False, stop=stop)


def hold(eng, sem, value, passed):
    eng.wait_ge(sem, value)
    eng.sem_inc(passed, 1)


def setup_block(nc, t, d):
    with ExitStack() as ctx:
        def sb(name, shape, dt=F32):
            return ctx.enter_context(nc.sbuf_tensor(name, shape, dt))

        def sem(name):
            return ctx.enter_context(nc.semaphore(name))

        c_row = sb("c_row", [B, H])
        c_silu = sb("c_silu", [B, H])
        c_T = sb("c_T", [P, KC, B])
        wmod = sb("wmod", [P, 2, KC, H])
        gate_row = sb("gate_row", [B, H])
        gate_abs = sb("gate_abs", [B, H])
        gate_sgn = sb("gate_sgn", [B, H])
        mod_rows = sb("mod_rows", [B, 4, H])
        mask_f = sb("mask_f", [P, P])
        rw_row = sb("rw_row", [RW, H])
        down_raw = sb("down_raw", [P, KC, DOWN])
        wq_up = sb("wq_up", [P, NH * HD])
        wq_up1 = sb("wq_up1", [QX, NH * HD])
        wk_up = sb("wk_up", [P, NH * HD])
        wv_up = sb("wv_up", [P, NH * HD])
        wqr = sb("wqr", [P, NH * RD])
        wqr1 = sb("wqr1", [P, NH * RD])
        wo = sb("wo", [P, NH // 2, H])
        head_T = sb("head_T", [P, 2, 4 * P])
        head_w = sb("head_w", [P, 2, SLOTS, P], F32R)

        ps = ctx.enter_context(nc.psum_tensor("ps_setup", [P, 8, 512], F32))
        T_PS, M_PS, O_PS, C_PS, R_PS = (0, 1), (2, 3), (4, 5), 6, 7

        c_loaded = sem("c_loaded")
        consts_loaded = sem("consts_loaded")
        tables_loaded = sem("tables_loaded")
        down_loaded = sem("down_loaded")
        wmod_loaded = [sem(f"wmod_loaded{j}") for j in range(2)]
        up_loaded = [sem(f"up_loaded{half}") for half in range(2)]
        wo_loaded = [sem(f"wo_loaded{quarter}") for quarter in range(NG)]
        rope_loaded = sem("rope_loaded")
        router_loaded = sem("router_loaded")
        c_exp_ready = sem("c_exp_ready")
        c_step = sem("c_step")
        c_T_mm = sem("c_T_mm")
        c_T_ready = sem("c_T_ready")
        mod_mm = sem("mod_mm")
        mod_taken = sem("mod_taken")
        gate_step = sem("gate_step")
        gates_ready = sem("gates_ready")
        gates_stored = sem("gates_stored")
        router_mm = sem("router_mm")
        down_hi = sem("down_hi")
        turned = sem("turned")
        turned_copied = sem("turned_copied")
        m_mm = sem("m_mm")
        o_mm = sem("o_mm")
        m_hi = sem("m_hi")
        m_lo = sem("m_lo")
        o_hi = sem("o_hi")
        o_lo = sem("o_lo")
        rope_hi = sem("rope_hi")
        rope_lo = sem("rope_lo")
        rope1_lo = sem("rope1_lo")
        head_stored = [sem(f"head_stored{par}") for par in range(2)]

        block = ctx.enter_context(nc.Block())

        def load_wo(sp, quarter):
            first = quarter * HG
            sp.dma_start(wo[:, first % (2 * HG):first % (2 * HG) + HG, :],
                         d["wo"].rearrange("(h p) n -> p h n", p=HD)[:, first:first + HG, :]).then_inc(
                wo_loaded[quarter], 16)

        @block.sync
        def _(sp):
            sp.dma_start(c_row[:, :], d["c"]).then_inc(c_loaded, 16)
            sp.dma_start(t["ident"][:, :], d["ident"]).then_inc(consts_loaded, 16)
            sp.dma_start(mask_f[:, :], d["mask"]).then_inc(consts_loaded, 16)
            for half in range(2):
                cols = slice(half * NH * HD // 2, (half + 1) * NH * HD // 2)
                sp.dma_start(wq_up[:, cols], d["wq_up"][0:P, cols]).then_inc(up_loaded[half], 16)
                sp.dma_start(wq_up1[:, cols], d["wq_up"][P:QR, cols]).then_inc(up_loaded[half], 16)
                sp.dma_start(wk_up[:, cols], d["wk_up"][:, cols]).then_inc(up_loaded[half], 16)
                sp.dma_start(wv_up[:, cols], d["wv_up"][:, cols]).then_inc(up_loaded[half], 16)
                load_wo(sp, half)
            for h in range(NH):
                sp.wait_ge(rope_lo, h + 1)
                sp.wait_ge(rope1_lo, 2 * h + 2)
                sp.wait_ge(m_lo, 2 * h + 2)
                sp.dma_start(r32(d["head_w"][h]), r32(head_w[:, h % 2, :, :].rearrange("p s c -> p (s c)"))).then_inc(
                    head_stored[h % 2], 16)
                if h in (HG - 1, 2 * HG - 1):
                    sp.wait_ge(o_mm, h + 1)
                    load_wo(sp, h // HG + 2)
            for par in range(2):
                sp.wait_ge(head_stored[par], 16 * NH // 2)

        @block.gpsimd
        def _(pool):
            for h in range(NH):
                cols = slice(h * RD, (h + 1) * RD)
                if h == 0:
                    pool.wait_ge(rope_loaded, 48)
                if h >= 2:
                    pool.wait_ge(head_stored[h % 2], 16 * (h // 2))
                for slot, raw in ((3, wqr), (5, wqr1)):
                    for half in range(2):
                        last = nc.gpsimd.tensor_copy(head_w[:, h % 2, slot, half * RD:(half + 1) * RD], raw[:, cols])
                last.then_inc(rope_hi, 1)
                pool.wait_ge(rope_hi, h + 1)
                for half in range(2):
                    out = slice(half * RD, (half + 1) * RD)
                    last = nc.gpsimd.tensor_tensor(head_w[:, h % 2, 4, out], wqr[:, cols],
                                                   r32(head_w[:, h % 2, 3, out]), ALU.subtract)
                last.then_inc(rope_lo, 1)

        @block.scalar
        def _(act):
            act.dma_start(wqr[:, :], d["wq_rope"][0:P, :]).then_inc(rope_loaded, 16)
            act.dma_start(wqr1[0:QX, :], d["wq_rope"][P:QR, :]).then_inc(rope_loaded, 16)
            act.dma_start(wqr1[QX:P, :], d["wq_rope"][P:QR, :]).then_inc(rope_loaded, 16)
            act.wait_ge(c_loaded, 16)
            nc.scalar.activation(c_silu[:, :], c_row[:, :], ACT.Exp, scale=-1.0).then_inc(c_exp_ready, 1)
            wmod_k = d["wmod"].rearrange("(k p) n -> p k n", p=P)
            for j in range(2):
                act.dma_start(wmod[:, j, :, :], wmod_k[:, :, j * H:(j + 1) * H]).then_inc(wmod_loaded[j], 16)
            wq, wkv, wkr = (d[k].rearrange("(k p) n -> p k n", p=P) for k in ("wq_down", "wkv_down", "wk_rope"))
            half = RD // 2
            pieces = [(0, wq, 0, QR), (QR, wq, P, QX), (2 * P, wkv, 0, KVR),
                      (3 * P, wkr, 0, RD), (3 * P + RD, wkr, half, half), (3 * P + RD + half, wkr, 0, half),
                      (4 * P, wkr, half, half), (4 * P + half, wkr, 0, half), (4 * P + RD, wkr, 0, RD)]
            for dst, src, at, width in pieces:
                act.dma_start(down_raw[:, :, dst:dst + width], src[:, :, at:at + width]).then_inc(down_loaded, 16)
            act.dma_start(rw_row[0:E, :], d["router_w"]).then_inc(router_loaded, 16)
            act.dma_start(rw_row[E:RW, :], d["sh_gate_w"].rearrange("n a -> a n")).then_inc(router_loaded, 16)
            for name in ("rope_q", "rope_kc", "rope_ks"):
                act.dma_start(t[name][:, :], d[name]).then_inc(tables_loaded, 16)
            for h in range(NH):
                act.wait_ge(m_mm, h + 1)
                if h >= 2:
                    act.wait_ge(head_stored[h % 2], 16 * (h // 2))
                nc.scalar.activation(head_w[:, h % 2, 0, :], ps[:, M_PS[h % 2], 0:P], ACT.Copy)
                nc.scalar.activation(head_w[:, h % 2, 2, :], ps[:, M_PS[h % 2], P:2 * P], ACT.Copy).then_inc(m_hi, 1)
                act.wait_ge(o_mm, h + 1)
                nc.scalar.activation(t["wo_hi"][:, h, :], ps[:, O_PS[h % 2], :], ACT.Copy).then_inc(o_hi, 1)
                if h < NMOD - 2:
                    act.wait_ge(mod_mm, h + 1)
                    act.dma_start(wmod[:, h % 2, :, :], wmod_k[:, :, (h + 2) * H:(h + 3) * H]).then_inc(
                        wmod_loaded[h % 2], 16)
            act.wait_ge(tables_loaded, 48)
            act.wait_ge(gates_ready, 2)
            act.dma_start(d["mod_rows"], mod_rows[:, :, :]).then_inc(gates_stored, 16)
            act.wait_ge(gates_stored, 16)

        def turn(pe, h):
            if h % (NH // 2) == 0:
                pe.wait_ge(up_loaded[h // (NH // 2)], 64)
            if h >= 2:
                pe.wait_ge(turned_copied, h - 1)
            cols = slice(h * HD, (h + 1) * HD)
            bank = T_PS[h % 2]
            ident = t["ident"]
            nc.tensor.transpose(ps[:, bank, 0:P], wq_up[:, cols], ident[:, :])
            nc.tensor.transpose(ps[:, bank, P:P + QX], wq_up1[:, cols], ident[0:QX, 0:QX])
            nc.tensor.transpose(ps[:, bank, P + QX:2 * P], wq_up1[:, cols], ident[0:QX, 0:QX])
            nc.tensor.transpose(ps[:, bank, 2 * P:3 * P], wk_up[:, cols], ident[:, :])
            nc.tensor.transpose(ps[:, bank, 3 * P:4 * P], wv_up[:, cols], ident[:, :]).then_inc(turned, 1)

        @block.tensor
        def _(pe):
            pe.wait_ge(consts_loaded, 32)
            pe.wait_ge(c_step, 3)
            for k in range(KC):
                last = nc.tensor.transpose(ps[:, C_PS, k * B:(k + 1) * B], c_silu[:, k * P:(k + 1) * P],
                                           t["ident"][0:B, 0:B])
            last.then_inc(c_T_mm, 1)
            turn(pe, 0)
            for h in range(NH):
                if h + 1 < NH:
                    turn(pe, h + 1)
                pe.wait_ge(turned_copied, h + 1)
                if h >= 2:
                    pe.wait_ge(m_lo, 2 * (h - 1))
                    pe.wait_ge(o_lo, h - 1)
                T = head_T[:, h % 2, :]
                nc.tensor.matmul(ps[:, M_PS[h % 2], 0:P], T[:, 0:P], T[:, 2 * P:3 * P], start=True, stop=True)
                nc.tensor.matmul(ps[:, M_PS[h % 2], P:2 * P], T[:, P:2 * P], T[:, 2 * P:3 * P],
                                 start=True, stop=True).then_inc(m_mm, 1)
                if h % HG == 0:
                    pe.wait_ge(wo_loaded[h // HG], 16)
                nc.tensor.matmul(ps[:, O_PS[h % 2], :], T[:, 3 * P:4 * P], wo[:, h % (2 * HG), :],
                                 start=True, stop=True).then_inc(o_mm, 1)
                if h < NMOD:
                    if h == 0:
                        pe.wait_ge(c_T_ready, 1)
                    else:
                        pe.wait_ge(mod_taken, h)
                    pe.wait_ge(wmod_loaded[h % 2], 16 * (h // 2 + 1))
                    if h >= 2:
                        for k in range(KC):
                            last = nc.tensor.matmul(ps[0:B, C_PS, :], c_T[:, k, :], wmod[:, h % 2, k, :],
                                                    start=(k == 0), stop=(k == KC - 1))
                    else:
                        for c in range(KC):
                            for k in range(KC):
                                last = nc.tensor.matmul(ps[:, C_PS, c * B:(c + 1) * B],
                                                        wmod[:, h % 2, k, c * P:(c + 1) * P], c_T[:, k, :],
                                                        start=(k == 0), stop=(k == KC - 1))
                    last.then_inc(mod_mm, 1)
                if h == NMOD:
                    pe.wait_ge(router_loaded, 32)
                    for k in range(KC):
                        last = nc.tensor.transpose(ps[:, R_PS, k * RW:(k + 1) * RW], rw_row[:, k * P:(k + 1) * P],
                                                   t["ident"][0:RW, 0:RW])
                    last.then_inc(router_mm, 1)

        def split_products(dve, h):
            dve.wait_ge(m_hi, h + 1)
            nc.vector.tensor_tensor(head_w[:, h % 2, 1, :], ps[:, M_PS[h % 2], 0:P], r32(head_w[:, h % 2, 0, :]),
                                    ALU.subtract).then_inc(m_lo, 1)
            nc.vector.tensor_tensor(head_w[QX:P, h % 2, 2, :], ps[QX:P, M_PS[h % 2], P:2 * P],
                                    r32(head_w[QX:P, h % 2, 2, :]), ALU.subtract).then_inc(m_lo, 1)
            dve.wait_ge(rope_hi, h + 1)
            for half in range(2):
                out = slice(half * RD, (half + 1) * RD)
                nc.vector.tensor_tensor(head_w[QX:P, h % 2, 5, out], wqr1[QX:P, h * RD:(h + 1) * RD],
                                        r32(head_w[QX:P, h % 2, 5, out]), ALU.subtract).then_inc(rope1_lo, 1)
            dve.wait_ge(o_hi, h + 1)
            nc.vector.tensor_tensor(t["wo_lo"][:, h, :], ps[:, O_PS[h % 2], :], r32(t["wo_hi"][:, h, :]),
                                    ALU.subtract).then_inc(o_lo, 1)

        def take_mod(dve, j):
            dve.wait_ge(mod_mm, j + 1)
            half, kind = j // 3, j % 3
            if j < 2:
                out = t["mod"][:, :, kind * KC:(kind + 1) * KC]
                nc.vector.tensor_scalar_add(out, ps[:, C_PS, 0:KC * B].rearrange("p (k b) -> p b k", b=B),
                                            float(kind)).then_inc(mod_taken, 1)
                return
            if kind < 2:
                nc.vector.tensor_scalar_add(mod_rows[:, 2 + kind, :], ps[0:B, C_PS, :], float(kind)).then_inc(
                    mod_taken, 1)
                return
            nc.vector.tensor_copy(gate_row[:, :], ps[0:B, C_PS, :]).then_inc(mod_taken, 1)
            dve.wait_ge(mod_taken, j + 1)
            nc.vector.scalar_tensor_tensor(gate_abs[:, :], gate_row[:, :], -1.0, gate_row[:, :],
                                           ALU.mult, ALU.max).then_inc(gate_step, 1)
            nc.vector.tensor_scalar(gate_sgn[:, :], gate_row[:, :], 0.0, 2.0, ALU.is_ge,
                                    ALU.mult).then_inc(gate_step, 1)
            dve.wait_ge(gate_step, 3 * half + 2)
            nc.vector.tensor_scalar_max(gate_abs[:, :], gate_abs[:, :], 0.25).then_inc(gate_step, 1)
            dve.wait_ge(gate_step, 3 * half + 3)
            nc.vector.scalar_tensor_tensor(mod_rows[:, half, :], gate_sgn[:, :], -1.0, gate_abs[:, :],
                                           ALU.add, ALU.mult).then_inc(gates_ready, 1)

        @block.vector
        def _(dve):
            nc.vector.memset(t["eps"][:, :], EPS)
            dve.wait_ge(c_exp_ready, 1)
            nc.vector.tensor_scalar_add(c_silu[:, :], c_silu[:, :], 1.0).then_inc(c_step, 1)
            dve.wait_ge(c_step, 1)
            nc.vector.reciprocal(c_silu[:, :], c_silu[:, :]).then_inc(c_step, 1)
            dve.wait_ge(c_step, 2)
            nc.vector.tensor_tensor(c_silu[:, :], c_row[:, :], c_silu[:, :], ALU.mult).then_inc(c_step, 1)
            dve.wait_ge(consts_loaded, 32)
            nc.vector.tensor_copy(t["mask"][:, :], mask_f[:, :])
            nc.vector.tensor_copy(t["ident_b"][:, :], t["ident"][:, :])
            dve.wait_ge(c_T_mm, 1)
            nc.vector.tensor_copy(c_T[:, :, :].rearrange("p k b -> p (k b)"), ps[:, C_PS, 0:KC * B]).then_inc(
                c_T_ready, 1)
            for h in range(NH):
                dve.wait_ge(turned, h + 1)
                if h >= 2:
                    dve.wait_ge(o_mm, h - 1)
                nc.vector.tensor_copy(head_T[:, h % 2, :], ps[:, T_PS[h % 2], :]).then_inc(turned_copied, 1)
                if h >= 1:
                    split_products(dve, h - 1)
                if 1 <= h <= NMOD:
                    take_mod(dve, h - 1)
                if h == NMOD + 1:
                    dve.wait_ge(router_mm, 1)
                    nc.vector.tensor_copy(t["router_T"][:, :, :].rearrange("p k e -> p (k e)"),
                                          ps[:, R_PS, 0:KC * RW])
                if h == 1:
                    dve.wait_ge(down_loaded, 16 * 9)
                if 1 <= h <= KC:
                    nc.vector.tensor_copy(t["down_hi"][:, h - 1, :], down_raw[:, h - 1, :]).then_inc(down_hi, 1)
                if 2 <= h <= KC + 1:
                    dve.wait_ge(down_hi, h - 1)
                    nc.vector.tensor_tensor(t["down_lo"][:, h - 2, :], down_raw[:, h - 2, :],
                                            r32(t["down_hi"][:, h - 2, :]), ALU.subtract)
            split_products(dve, NH - 1)


def attention_block(nc, t, d):
    with ExitStack() as ctx:
        def sb(name, shape, dt=F32):
            return ctx.enter_context(nc.sbuf_tensor(name, shape, dt))

        def sem(name):
            return ctx.enter_context(nc.semaphore(name))

        xt = sb("xt", [P, TT, H])
        probs = sb("probs", [P, 2, TT, L])
        full1 = rows = probs[:, 1, :, :]
        full2 = probs[:, 0, :, :]
        xn = sb("xn", [P, TT, H])
        ctx_hi = sb("ctx_hi", [P, HG, L], F32R)
        ctx_lo = sb("ctx_lo", [P, HG, L], F32R)
        h2_hi, h2_lo = ctx_hi, ctx_lo
        stats = sb("stats", [P, TT, 6])
        mv = sb("mv", [P, 2, TT, 2])
        std = sb("std", [P, 2, TT])
        rstd = sb("rstd", [P, 2, TT])
        mod_b = sb("mod_b", [P, 2 * KC])
        ga_b = sb("ga_b", [P, H])
        q0_hi = sb("q0_hi", [P, L], F32R)
        q0_lo = sb("q0_lo", [P, L], F32R)
        q1_hi2 = sb("q1_hi2", [P, L], F32R)
        q1_lo = sb("q1_lo", [QX, L], F32R)
        kv_hi = sb("kv_hi", [P, L], F32R)
        kv_lo = sb("kv_lo", [P, L], F32R)
        kr_hi = sb("kr_hi", [P, L], F32R)
        kr_lo = sb("kr_lo", [P, L], F32R)
        v_hi = sb("v_hi", [P, TT, KVR], F32R)
        v_lo = sb("v_lo", [P, TT, KVR], F32R)
        head_w = sb("head_w_in", [P, 2, SLOTS, P], F32R)
        qc_hi = sb("qc_hi", [P, 2, L], F32R)
        mod2 = r32(qc_hi[:, :, :])
        qc_lo = sb("qc_lo", [P, 2, L], F32R)
        qr_full = sb("qr_full", [P, L])
        qr_hi = sb("qr_hi", [P, 2, L], F32R)
        qr_lo = sb("qr_lo", [P, 2, L], F32R)
        mx = sb("mx", [P, 2, TT])
        nmx = sb("nmx", [P, 2, TT])
        sums = sb("sums", [P, 2, TT])
        rsum = sb("rsum", [P, 2, TT])
        pt_hi = sb("pt_hi", [P, TT, L], F32R)
        pt_lo = sb("pt_lo", [P, TT, L], F32R)
        h_hi, h_lo = pt_hi, pt_lo
        gated = sb("gated", [P, 2, H])

        ps = ctx.enter_context(nc.psum_tensor("ps_attn", [P, 8, 512], F32))
        QC, QRP, S0, PT, CT = 0, 1, 2, 6, 7
        PROJ = [0, 1, 6, 7, 2]
        TURN = [PT + i % 2 for i in range(TT)]

        x_loaded = sem("x_loaded")
        ga_loaded = sem("ga_loaded")
        head_loaded = [sem(f"head_loaded{par}") for par in range(2)]
        x1_stored = sem("x1_stored")
        h2_stored = sem("h2_stored")
        mod_loaded = sem("mod_loaded")
        scaled_ready = sem("scaled_ready")
        rows_ready = sem("rows_ready")
        stats_ready = sem("stats_ready")
        mv_ready = sem("mv_ready")
        xn_loaded = sem("xn_loaded")
        std_ready = sem("std_ready")
        rstd_ready = sem("rstd_ready")
        xn_ready = sem("xn_ready")
        rows_stored = sem("rows_stored")
        normed_T = sem("normed_T")
        mod_ready = sem("mod_ready")
        full_ready = sem("full_ready")
        h_hi_ready = sem("h_hi_ready")
        h_lo_ready = sem("h_lo_ready")
        proj_mm = sem("proj_mm")
        lat_hi = sem("lat_hi")
        lat_lo = sem("lat_lo")
        kv_full_ready = sem("kv_full_ready")
        kr_parts = sem("kr_parts")
        kr_full_ready = sem("kr_full_ready")
        kr_lo_ready = sem("kr_lo_ready")
        v_T = sem("v_T")
        zeros_ready = sem("zeros_ready")
        passed = sem("passed")
        qr_mm = sem("qr_mm")
        qc_mm = sem("qc_mm")
        qr_full_ready = sem("qr_full_ready")
        qr_hi_ready = sem("qr_hi_ready")
        qr_lo_ready = sem("qr_lo_ready")
        qc_hi_ready = sem("qc_hi_ready")
        qc_lo_ready = sem("qc_lo_ready")
        scores_mm = sem("scores_mm")
        mx_ready = sem("mx_ready")
        nmx_ready = sem("nmx_ready")
        exp_done = sem("exp_done")
        rsum_ready = sem("rsum_ready")
        probs_ready = sem("probs_ready")
        probs_T = sem("probs_T")
        pt_hi_ready = sem("pt_hi_ready")
        pt_lo_ready = sem("pt_lo_ready")
        ctx_mm = sem("ctx_mm")
        ctx_hi_ready = sem("ctx_hi_ready")
        ctx_lo_ready = sem("ctx_lo_ready")
        out_mm = sem("out_mm")
        gated_ready = sem("gated_ready")
        x_added = sem("x_added")
        logits_mm = sem("logits_mm")
        logits_ready = sem("logits_ready")

        seeded = (x1_stored, gated_ready, qc_mm, h2_stored, rows_stored, qr_full_ready, qc_lo_ready, exp_done, pt_lo_ready, ctx_lo_ready, logits_ready, logits_mm, h_lo_ready, qr_lo_ready, ctx_mm, out_mm)
        with nc.Block() as seeds:
            @seeds.gpsimd
            def _(pool):
                for semaphore in seeded:
                    pool.sem_inc(semaphore, 1)

        def after(eng, semaphore, n):
            eng.wait_ge(semaphore, n + 1)

        block = ctx.enter_context(nc.Block())

        def steps(eng, b, step):
            step(b, 0, 0, first=True)
            with eng.Fori(0, NG - 1) as g:
                for j in range(1, HG + 1):
                    step(b, g * HG + j, j)
            for j in range(1, HG + 1):
                step(b, (NG - 1) * HG + j, j, last=(j >= HG - 1), tail=(j == HG), ending=True)

        def at_head(b, k):
            return b * NH + k

        @block.sync
        def _(sp):
            def batch(b, last=False):
                hold(sp, gated_ready, 1 + b * (NG * TT), passed)
                sp.dma_start(ga_b[:, :], d["mod_rows"][bass.ds(b, 1), 0, :].to_broadcast([P, H])).then_inc(ga_loaded, 16)
                for h in range(2):
                    hold(sp, qc_mm, 1 + at_head(b, 0), passed)
                    sp.dma_start(r32(head_w[:, h, :, :].rearrange("p s c -> p (s c)")),
                                 r32(d["head_w"][h])).then_inc(head_loaded[h], 16)
                hold(sp, x1_stored, 1 + b * 16, passed)
                sp.dma_start(xt[:, :, :], d["x"][bass.ds(b, 1)].rearrange("a (t p) n -> p (a t) n", p=P)).then_inc(
                    x_loaded, 16)
                with sp.Fori(1, NH // 2) as pair:
                    for h in range(2):
                        hold(sp, qc_mm, 1 + at_head(b, pair * 2 + (h - 1)), passed)
                        sp.dma_start(r32(head_w[:, h, :, :].rearrange("p s c -> p (s c)")),
                                     r32(d["head_w"][bass.ds(pair * 2 + h, 1)].rearrange("a p s -> (a p) s"))
                                     ).then_inc(head_loaded[h], 16)
                hold(sp, normed_T, b * (2 * KC) + KC, passed)
                sp.dma_start(xn[:, :, :], d["x"][bass.ds(0 if last else b + 1, 1)].rearrange(
                    "a (t p) n -> p (a t) n", p=P)).then_inc(xn_loaded, 16)
                hold(sp, scores_mm, b * (NH * TT) + NH * TT, passed)
                for row in range(2):
                    sp.dma_start(mod2[:, row, :], d["mod_rows"][bass.ds(b, 1), 2 + row, :].to_broadcast([P, H])
                                 ).then_inc(mod_loaded, 16)
                hold(sp, x_added, b * (NG * TT) + NG * TT, passed)
                sp.dma_start(d["x1"][bass.ds(b, 1)].rearrange("a (t p) n -> p (a t) n", p=P),
                             xt[:, :, :]).then_inc(x1_stored, 16)
                hold(sp, rows_ready, b * TT + TT, passed)
                sp.dma_start(d["h2_rows"][bass.ds(b * L, L)].rearrange("(t p) n -> p t n", p=P),
                             rows).then_inc(rows_stored, 16)
                for part, ready, name in ((h2_hi, h_hi_ready, "h2_hi"), (h2_lo, h_lo_ready, "h2_lo")):
                    hold(sp, ready, (ready is h_lo_ready) + b * (2 * KC) + 2 * KC, passed)
                    sp.dma_start(r32(d[name][:, :, bass.ds(b * L, L)].rearrange("c p n -> p c n")),
                                 r32(part[:, :, :])).then_inc(h2_stored, 16)

            sp.dma_start(xn[:, :, :], d["x"][0].rearrange("(t p) n -> p t n", p=P)).then_inc(xn_loaded, 16)
            with sp.Fori(0, B - 1) as b:
                batch(b)
            batch(B - 1, last=True)
            after(sp, x1_stored, 16 * B)
            after(sp, rows_stored, 16 * B)
            after(sp, h2_stored, 32 * B)

        @block.gpsimd
        def _(pool):
            def normalize_xn(tiles):
                for i in tiles:
                    nc.gpsimd.tensor_scalar(xn[:, i, :], xn[:, i, :], mv[:, 0, i, 0:1], rstd[:, 0, i:i + 1],
                                            ALU.subtract, ALU.mult).then_inc(xn_ready, 1)

            def h_lows(r, lo, full, hi):
                for c in range(1, KC, 2):
                    pool.wait_ge(h_hi_ready, r * KC + (c + 1))
                    nc.gpsimd.tensor_tensor(lo[:, c, :], full[:, c, :], r32(hi[:, c, :]),
                                            ALU.subtract).then_inc(h_lo_ready, 1)

            def rope_low(b, k, par):
                n = at_head(b, k)
                pool.wait_ge(qr_hi_ready, n + 1)
                nc.gpsimd.tensor_tensor(qr_lo[:, par, :], qr_full[:, :], r32(qr_hi[:, par, :]),
                                        ALU.subtract).then_inc(qr_lo_ready, 1)

            def step(b, k, j, first=False, last=False, tail=False, ending=False):
                if not last:
                    rope_low(b, k + 1, (j + 1) % 2)
                if tail:
                    hold(pool, rstd_ready, b * (1 + TT) + 2, passed)
                if j == HG:
                    for tile in range(TT):
                        done = at_head(b, k) - HG + tile
                        after(pool, gated_ready, done + 1)
                        nc.gpsimd.tensor_tensor(xt[:, tile, :], xt[:, tile, :], gated[:, tile % 2, :],
                                                ALU.add).then_inc(x_added, 1)
                        if tail:
                            normalize_xn((tile,))

            pool.wait_ge(rstd_ready, 1)
            normalize_xn(range(TT))
            with pool.Fori(0, B) as b:
                h_lows(b * 2, h_lo, full1, h_hi)
                pool.wait_ge(kr_parts, b * 2 + 2)
                nc.gpsimd.tensor_tensor(full1[:, 3, :], full1[:, 1, :], full1[:, 2, :], ALU.add).then_inc(
                    kr_full_ready, 1)
                pool.wait_ge(lat_hi, b * 5 + 5)
                nc.gpsimd.tensor_tensor(kr_lo[:, :], full1[:, 3, :], r32(kr_hi[:, :]), ALU.subtract).then_inc(
                    kr_lo_ready, 1)
                for part in (pt_hi, pt_lo):
                    nc.gpsimd.memset(r32(part[:, TT - 1, (TT - 2) * P:(TT - 1) * P]), 0.0).then_inc(zeros_ready, 1)
                rope_low(b, 0, 0)
                steps(pool, b, step)
                h_lows(b * 2 + 1, h2_lo, full2, h2_hi)

        @block.scalar
        def _(act):
            def deviation(norm, tiles, done):
                act.wait_ge(mv_ready, done)
                nc.scalar.activation(std[:, norm, tiles], mv[:, norm, tiles, 1], ACT.Sqrt, bias=t["eps"][:, :]
                                     ).then_inc(std_ready, 1)

            def h_highs(r, hi, full):
                for c in range(KC):
                    act.wait_ge(full_ready, r * KC + (c + 1))
                    nc.scalar.activation(hi[:, c, :], full[:, c, :], ACT.Copy).then_inc(h_hi_ready, 1)

            def query_high(b, k, par):
                after(act, qc_mm, at_head(b, k) + 1)
                nc.scalar.activation(qc_hi[:, par, :], ps[:, QC, :], ACT.Copy).then_inc(qc_hi_ready, 1)

            def probs_high(b, k, i):
                done = at_head(b, k) * TT
                act.wait_ge(probs_T, done + (i + 1))
                if i == 0:
                    after(act, ctx_mm, at_head(b, k))
                nc.scalar.activation(pt_hi[:, 0:i + 1, i * P:(i + 1) * P],
                                     ps[:, TURN[i], 0:(i + 1) * P].rearrange("p (k q) -> p k q", q=P),
                                     ACT.Copy).then_inc(pt_hi_ready, 1)

            def exps(b, k, par, i):
                act.wait_ge(nmx_ready, at_head(b, k) * TT + (i + 1))
                nc.scalar.activation(probs[:, par, i, 0:(i + 1) * P], ps[:, S0 + i, 0:(i + 1) * P], ACT.Exp,
                                     bias=nmx[:, par, i:i + 1], scale=SCALE,
                                     accum_out=sums[:, par, i:i + 1]).then_inc(exp_done, 1)

            def step(b, k, j, first=False, last=False, tail=False, ending=False):
                for i in range(TT):
                    if i == TT - 1 and not last:
                        query_high(b, k + 1, (j + 1) % 2)
                    if not first:
                        probs_high(b, k - 1, i)
                    if not tail:
                        exps(b, k, j % 2, i)
                if not first:
                    after(act, ctx_mm, at_head(b, k))
                    if j == 1:
                        after(act, out_mm, at_head(b, k) - 1)
                    nc.scalar.activation(ctx_hi[:, j - 1, :], ps[:, CT, :], ACT.Copy).then_inc(ctx_hi_ready, 1)

            deviation(0, slice(0, TT), TT)
            with act.Fori(0, B) as b:
                h_highs(b * 2, h_hi, full1)
                for m, (out, bank) in enumerate(((q0_hi[:, :], 0), (q1_hi2[:, :], 1), (kv_hi[:, :], 6))):
                    act.wait_ge(proj_mm, b * 5 + (m + 1))
                    nc.scalar.activation(out, ps[:, bank, :], ACT.Copy).then_inc(lat_hi, 1)
                act.wait_ge(v_T, b + 1)
                nc.scalar.activation(v_hi[:, :, :].rearrange("p t c -> p (t c)"), ps[:, 3, :], ACT.Copy).then_inc(
                    lat_hi, 1)
                act.wait_ge(kr_full_ready, b + 1)
                nc.scalar.activation(kr_hi[:, :], full1[:, 3, :], ACT.Copy).then_inc(lat_hi, 1)
                query_high(b, 0, 0)
                after(act, h2_stored, b * 32)
                steps(act, b, step)
                deviation(0, slice(0, TT), b * (2 * TT) + 2 * TT)
                for i in range(TT):
                    deviation(1, slice(i, i + 1), b * (2 * TT) + 2 * TT + (i + 1))
                h_highs(b * 2 + 1, h2_hi, full2)
                hold(act, logits_mm, 1 + b + 1, passed)
                nc.scalar.activation(t["logits"][:, bass.ds(b * TT, TT), :].rearrange("p t e -> p (t e)"),
                                     ps[:, PT, 0:TT * RW], ACT.Copy).then_inc(logits_ready, 1)

        @block.tensor
        def _(pe):
            def turn(tokens, i):
                for c in range(KC):
                    ins = nc.tensor.transpose(ps[:, S0 + c, i * P:(i + 1) * P], tokens[:, i, c * P:(c + 1) * P],
                                              t["ident"][:, :])
                    if i == TT - 1:
                        ins.then_inc(normed_T, 1)

            def queries(b, k, par):
                n = at_head(b, k)
                pe.wait_ge(head_loaded[par], n * 8 + (16 - 8 * par))
                for bank, slot, mm, free in ((QRP, 3, qr_mm, qr_full_ready), (QC, 0, qc_mm, qc_lo_ready)):
                    after(pe, free, n)
                    three(nc, ps[:, bank, :], head_w[:, par, slot, :], head_w[:, par, slot + 1, :], q0_hi[:, :],
                          q0_lo[:, :], True, False)
                    nc.tensor.matmul(ps[:, bank, :], head_w[:, par, slot + 2, :], q1_hi2[:, :], start=False,
                                     stop=False)
                    nc.tensor.matmul(ps[:, bank, :], head_w[0:QX, par, slot + 2, :], q1_lo[:, :], start=False,
                                     stop=True).then_inc(mm, 1)

            def score(b, k, par, i, first):
                n = at_head(b, k)
                if i == 0:
                    after(pe, qc_lo_ready, n + 1)
                    after(pe, qr_lo_ready, n + 1)
                after(pe, exp_done, n * TT if first else n * TT + (i + 1 - TT))
                out = ps[:, S0 + i, 0:WIDTH[i]]
                q, keys = slice(i * P, (i + 1) * P), slice(0, WIDTH[i])
                three(nc, out, qc_hi[:, par, q], qc_lo[:, par, q], kv_hi[:, keys], kv_lo[:, keys], True, False)
                nc.tensor.matmul(ps[:, S0 + i, i * P:(i + 1) * P], t["ident_b"][:, :], t["mask"][:, :], start=False,
                                 stop=False, skip_group_check=True)
                three(nc, out, qr_hi[:, par, q], qr_lo[:, par, q], kr_hi[:, keys], kr_lo[:, keys], False,
                      True).then_inc(scores_mm, 1)

            def turn_probs(b, k, par, i, after_out=False):
                n = at_head(b, k)
                pe.wait_ge(probs_ready, n * TT + (i + 1))
                if i >= 2:
                    after(pe, pt_lo_ready, n * TT + (i - 1))
                if i == 1:
                    after(pe, ctx_lo_ready, n)
                if after_out:
                    after(pe, gated_ready, n)
                for c in range(i + 1):
                    last = nc.tensor.transpose(ps[:, TURN[i], c * P:(c + 1) * P], probs[:, par, i, c * P:(c + 1) * P],
                                               t["ident"][:, :])
                last.then_inc(probs_T, 1)

            def context(b, k):
                n = at_head(b, k)
                after(pe, pt_lo_ready, n * TT + TT)
                after(pe, ctx_lo_ready, n)
                nc.tensor.matmul(ps[:, CT, :], v_hi[:, 0, :], pt_hi[:, 0, :], start=True, stop=False)
                nc.tensor.matmul(ps[:, CT, :], v_hi[:, 0, :], pt_lo[:, 0, :], start=False, stop=False)
                for c in range(1, TT):
                    first_q = min(c, TT - 2) * P
                    three(nc, ps[:, CT, first_q:], v_hi[:, c, :], v_lo[:, c, :], pt_hi[:, c, first_q:],
                          pt_lo[:, c, first_q:], False, False)
                nc.tensor.matmul(ps[:, CT, :], v_lo[:, 0, :], pt_hi[:, 0, :], start=False,
                                 stop=True).then_inc(ctx_mm, 1)

            def project_out(b, k):
                n = at_head(b, k)
                after(pe, ctx_lo_ready, n)
                for tile in range(TT):
                    bank = PT + tile % 2
                    if tile >= 2:
                        after(pe, gated_ready, n - HG + (tile - 1))
                    for j in range(HG):
                        q = slice(tile * P, (tile + 1) * P)
                        head = bass.ds(k + (j - HG), 1)
                        w_hi, w_lo = (t[w][:, head, :].rearrange("p a n -> p (a n)") for w in ("wo_hi", "wo_lo"))
                        nc.tensor.matmul(ps[:, bank, :], ctx_hi[:, j, q], w_hi, start=(j == 0), stop=False)
                        nc.tensor.matmul(ps[:, bank, :], ctx_hi[:, j, q], w_lo, start=False, stop=False)
                        last = nc.tensor.matmul(ps[:, bank, :], ctx_lo[:, j, q], w_hi, start=False,
                                                stop=(j == HG - 1))
                    last.then_inc(out_mm, 1)

            def step(b, k, j, first=False, last=False, tail=False, ending=False):
                for i in range(TT):
                    if i == TT - 1 and not last:
                        queries(b, k + 1, (j + 1) % 2)
                    if not first:
                        turn_probs(b, k - 1, (j - 1) % 2, i, after_out=(j == 1 and i == 0))
                    if not tail:
                        score(b, k, j % 2, i, first)
                if not first:
                    context(b, k - 1)
                if j == HG:
                    project_out(b, k)

            for i in range(TT):
                pe.wait_ge(xn_ready, i + 1)
                turn(xn, i)
            with pe.Fori(0, B) as b:
                after(pe, h_lo_ready, b * (2 * KC) + KC)
                after(pe, logits_ready, b)
                for m, bank in enumerate(PROJ):
                    cols = slice(m * P, (m + 1) * P)
                    for c in range(KC):
                        last = three(nc, ps[:, bank, :], t["down_hi"][:, c, cols], t["down_lo"][:, c, cols],
                                     h_hi[:, c, :], h_lo[:, c, :], c == 0, c == KC - 1)
                    last.then_inc(proj_mm, 1)
                pe.wait_ge(kv_full_ready, b + 1)
                for i in range(TT):
                    last = nc.tensor.transpose(ps[:, 3, i * P:(i + 1) * P], full1[:, 0, i * P:(i + 1) * P],
                                               t["ident"][:, :])
                last.then_inc(v_T, 1)
                pe.wait_ge(lat_lo, b * 4 + 2)
                queries(b, 0, 0)
                pe.wait_ge(lat_lo, b * 4 + 4)
                pe.wait_ge(kr_lo_ready, b + 1)
                pe.wait_ge(zeros_ready, b * 2 + 2)
                steps(pe, b, step)
                for i in range(TT):
                    pe.wait_ge(rows_ready, b * TT + (i + 1))
                    turn(rows, i)
                pe.wait_ge(full_ready, b * (2 * KC) + 2 * KC)
                for i in range(TT):
                    pe.wait_ge(xn_ready, b * TT + (TT + i + 1))
                    turn(xn, i)
                after(pe, gated_ready, b * (NG * TT) + NG * TT)
                for i in range(TT):
                    for c in range(KC):
                        last = nc.tensor.matmul(ps[:, PT, i * RW:(i + 1) * RW], full2[:, c, i * P:(i + 1) * P],
                                                t["router_T"][:, c, :], start=(c == 0), stop=(c == KC - 1))
                last.then_inc(logits_mm, 1)

        @block.vector
        def _(dve):
            def statistics(src, norm, i, n):
                nc.vector.bn_stats(stats[:, i, :], src[:, i, :]).then_inc(stats_ready, 1)
                hold(dve, stats_ready, n + (i + 1), passed)
                nc.vector.bn_aggr(mv[:, norm, i, :], stats[:, i, :]).then_inc(mv_ready, 1)

            def inverse(norm, tiles, done):
                dve.wait_ge(std_ready, done)
                nc.vector.reciprocal(rstd[:, norm, tiles], std[:, norm, tiles]).then_inc(rstd_ready, 1)

            def h_low(r, c, lo, full, hi):
                dve.wait_ge(h_hi_ready, r * KC + (c + 1))
                nc.vector.tensor_tensor(lo[:, c, :], full[:, c, :], r32(hi[:, c, :]), ALU.subtract).then_inc(
                    h_lo_ready, 1)

            def take_first(b):
                for c in range(KC):
                    dve.wait_ge(normed_T, b * (2 * KC) + (c + 1))
                    nc.vector.tensor_scalar(full1[:, c, :], ps[:, S0 + c, :], mod_b[:, KC + c:KC + c + 1],
                                            mod_b[:, c:c + 1], ALU.mult, ALU.add).then_inc(full_ready, 1)
                    if c == 1:
                        after(dve, h_lo_ready, b * (2 * KC))
                    if c % 2 == 1:
                        h_low(b * 2, c - 1, h_lo, full1, h_hi)

            def take_second(b):
                for c in range(KC):
                    dve.wait_ge(normed_T, b * (2 * KC) + (KC + c + 1))
                    nc.vector.tensor_copy(full2[:, c, :], ps[:, S0 + c, :]).then_inc(full_ready, 1)
                    if c == 1:
                        after(dve, h_lo_ready, b * (2 * KC) + KC)
                    if c % 2 == 1:
                        h_low(b * 2 + 1, c - 1, h2_lo, full2, h2_hi)

            def finish_rows(b, tile):
                at = b * (2 * TT) + 2 * TT
                done = (b * NH + NH) - HG + tile
                dve.wait_ge(x_added, done + 1)
                statistics(xt, 1, tile, at)
                dve.wait_ge(mv_ready, at + (tile + 1))
                if tile == 0:
                    dve.wait_ge(mod_loaded, b * 32 + 32)
                nc.vector.scalar_tensor_tensor(rows[:, tile, :], xt[:, tile, :], mv[:, 1, tile, 0:1], mod2[:, 1, :],
                                               ALU.subtract, ALU.mult).then_inc(scaled_ready, 1)
                done = b * (1 + TT) + (2 + tile + 1)
                inverse(1, slice(tile, tile + 1), done)
                dve.wait_ge(rstd_ready, done)
                dve.wait_ge(scaled_ready, b * TT + (tile + 1))
                nc.vector.scalar_tensor_tensor(rows[:, tile, :], rows[:, tile, :], rstd[:, 1, tile:tile + 1],
                                               mod2[:, 0, :], ALU.mult, ALU.add).then_inc(rows_ready, 1)

            def low(out, bank, hi, ready):
                nc.vector.tensor_tensor(out, bank, r32(hi), ALU.subtract).then_inc(ready, 1)

            def query_rope(b, k, par):
                n = at_head(b, k)
                dve.wait_ge(qr_mm, n + 1)
                after(dve, qr_lo_ready, n)
                nc.vector.tensor_tensor(qr_full[:, :], ps[:, QRP, :], t["rope_q"][:, :], ALU.mult).then_inc(
                    qr_full_ready, 1)
                after(dve, qr_full_ready, n + 1)
                nc.vector.tensor_copy(qr_hi[:, par, :], qr_full[:, :]).then_inc(qr_hi_ready, 1)
                dve.wait_ge(qc_hi_ready, n + 1)
                low(qc_lo[:, par, :], ps[:, QC, :], qc_hi[:, par, :], qc_lo_ready)

            def probs_low(b, k, i):
                dve.wait_ge(pt_hi_ready, at_head(b, k) * TT + (i + 1))
                out = (slice(None), slice(0, i + 1), slice(i * P, (i + 1) * P))
                low(pt_lo[out], ps[:, TURN[i], 0:(i + 1) * P].rearrange("p (k q) -> p k q", q=P), pt_hi[out],
                    pt_lo_ready)

            def maxima(b, k, par, i):
                done = at_head(b, k) * TT
                dve.wait_ge(scores_mm, done + (i + 1))
                nc.vector.reduce_max(mx[:, par, i:i + 1], ps[:, S0 + i, 0:(i + 1) * P], AX.X).then_inc(mx_ready, 1)
                dve.wait_ge(mx_ready, done + (i + 1))
                nc.vector.tensor_scalar(nmx[:, par, i:i + 1], mx[:, par, i:i + 1], -SCALE, None,
                                        ALU.mult).then_inc(nmx_ready, 1)

            def normalize(b, k, par, i):
                done = at_head(b, k) * TT
                after(dve, exp_done, done + (i + 1))
                nc.vector.reciprocal(rsum[:, par, i:i + 1], sums[:, par, i:i + 1]).then_inc(rsum_ready, 1)
                dve.wait_ge(rsum_ready, done + (i + 1))
                nc.vector.tensor_scalar(probs[:, par, i, 0:(i + 1) * P], probs[:, par, i, 0:(i + 1) * P],
                                        rsum[:, par, i:i + 1], None, ALU.mult).then_inc(probs_ready, 1)

            def step(b, k, j, first=False, last=False, tail=False, ending=False):
                for i in range(TT):
                    if i == TT - 1 and not last:
                        query_rope(b, k + 1, (j + 1) % 2)
                    if not first:
                        probs_low(b, k - 1, i)
                    if not tail:
                        maxima(b, k, j % 2, i)
                        if i > 0:
                            normalize(b, k, j % 2, i - 1)
                if not tail:
                    normalize(b, k, j % 2, TT - 1)
                if ending and not tail and j >= HG - 2:
                    if j == HG - 2:
                        dve.wait_ge(xn_loaded, b * 16 + 32)
                    for i in range((j - HG + 2) * TT // 2, (j - HG + 3) * TT // 2):
                        statistics(xn, 0, i, b * (2 * TT) + TT)
                if not first:
                    dve.wait_ge(ctx_hi_ready, at_head(b, k))
                    low(ctx_lo[:, j - 1, :], ps[:, CT, :], ctx_hi[:, j - 1, :], ctx_lo_ready)
                if tail:
                    inverse(0, slice(0, TT), b * (1 + TT) + 2)
                if j == HG:
                    for tile in range(TT):
                        done = at_head(b, k) - HG + tile
                        after(dve, out_mm, done + 1)
                        if tile >= 2:
                            dve.wait_ge(x_added, done - 1)
                        nc.vector.tensor_tensor(gated[:, tile % 2, :], ps[:, PT + tile % 2, :], ga_b[:, :],
                                                ALU.mult).then_inc(gated_ready, 1)
                        if tail and tile >= 1:
                            finish_rows(b, tile - 1)
                    if tail:
                        finish_rows(b, TT - 1)

            dve.wait_ge(xn_loaded, 16)
            for i in range(TT):
                statistics(xn, 0, i, 0)
            inverse(0, slice(0, TT), 1)
            with dve.Fori(0, B) as b:
                nc.vector.tensor_copy(mod_b[:, :], t["mod"][:, bass.ds(b, 1), :].rearrange("p a k -> p (a k)")
                                      ).then_inc(mod_ready, 1)
                dve.wait_ge(mod_ready, b + 1)
                after(dve, rows_stored, b * 16)
                take_first(b)
                dve.wait_ge(lat_hi, b * 5 + 1)
                low(q0_lo[:, :], ps[:, 0, :], q0_hi[:, :], lat_lo)
                dve.wait_ge(lat_hi, b * 5 + 2)
                low(q1_lo[:, :], ps[0:QX, 1, :], q1_hi2[0:QX, :], lat_lo)
                dve.wait_ge(lat_hi, b * 5 + 3)
                nc.vector.tensor_copy(full1[:, 0, :], ps[:, 6, :]).then_inc(kv_full_ready, 1)
                low(kv_lo[:, :], ps[:, 6, :], kv_hi[:, :], lat_lo)
                dve.wait_ge(proj_mm, b * 5 + 5)
                nc.vector.tensor_tensor(full1[:, 1, :], ps[:, 7, :], t["rope_kc"][:, :], ALU.mult).then_inc(kr_parts, 1)
                nc.vector.tensor_tensor(full1[:, 2, :], ps[:, 2, :], t["rope_ks"][:, :], ALU.mult).then_inc(kr_parts, 1)
                dve.wait_ge(lat_hi, b * 5 + 4)
                low(v_lo[:, :, :].rearrange("p t c -> p (t c)"), ps[:, 3, :], v_hi[:, :, :].rearrange("p t c -> p (t c)"),
                    lat_lo)
                dve.wait_ge(ga_loaded, b * 16 + 16)
                dve.wait_ge(x_loaded, b * 16 + 16)
                query_rope(b, 0, 0)
                steps(dve, b, step)
                take_second(b)


def block_kernel(nc, d):
    with ExitStack() as outer:
        def sb(name, shape, dt=F32):
            return outer.enter_context(nc.sbuf_tensor(name, shape, dt))

        t = {"logits": sb("logits", [P, NT, RW])}
        with ExitStack() as attn:
            def sa(name, shape, dt=F32):
                t[name] = attn.enter_context(nc.sbuf_tensor(name, shape, dt))

            sa("ident", [P, P])
            sa("eps", [P, 1])
            sa("ident_b", [P, P], BF16)
            sa("mask", [P, P], BF16)
            sa("rope_q", [P, L])
            sa("rope_kc", [P, L])
            sa("rope_ks", [P, L])
            sa("mod", [P, B, 2 * KC])
            sa("router_T", [P, KC, RW])
            sa("down_hi", [P, KC, DOWN], F32R)
            sa("down_lo", [P, KC, DOWN], F32R)
            sa("wo_hi", [P, NH, H], F32R)
            sa("wo_lo", [P, NH, H], F32R)
            setup_block(nc, t, d)
            attention_block(nc, t, d)
        moe_block(nc, t, d)


def shape_constants():
    import numpy as np
    inv_freq = (1.0 / np.float32(10000.0) ** (np.arange(0, RD, 2, dtype=np.float32) / np.float32(RD))).astype(np.float32)
    freqs = np.outer(np.arange(L, dtype=np.float32), inv_freq).astype(np.float32).T
    cos, sin = np.cos(freqs), np.sin(freqs)
    return {
        "ident": np.eye(P, dtype=np.float32),
        "expert_ids": np.tile(np.arange(E, dtype=np.float32), (P, 1)),
        "tri": np.triu(np.ones((P, P), np.float32), 1),
        "tile_no": np.tile(np.arange(TILES, dtype=np.float32), (P, 1)),
        "tile_starts": np.tile(np.arange(0, N, TS, dtype=np.float32), (P, 1)),
        "token_pairs": np.stack([np.broadcast_to(np.arange(N, dtype=np.int32).reshape(NT, P).T[:, :, None],
                                                 (P, NT, TOPK)), np.zeros((P, NT, TOPK), np.int32)],
                                axis=-1).reshape(P, -1),
        "mask": np.triu(np.full((P, P), MASKED, np.float32), 1),
        "rope_q": np.concatenate([cos, cos, sin, sin]),
        "rope_kc": np.concatenate([cos, cos, cos, -cos]),
        "rope_ks": np.concatenate([-sin, sin, sin, sin]),
    }


def shared_block(nc, t, d):
    with ExitStack() as ctx:
        def sb(name, shape, dt=F32):
            return ctx.enter_context(nc.sbuf_tensor(name, shape, dt))

        def sem(name):
            return ctx.enter_context(nc.semaphore(name))

        BLOCKS = NS * B
        RING = NI + 1
        PIECES = KC + NI
        acc = t["acc"]
        h_hi = sb("h2_hi", [P, KC, N], F32R)
        h_lo = sb("h2_lo", [P, KC, N], F32R)
        gu_hi = sb("gu_hi", [P, 2, KC, 2 * IM], F32R)
        gu_lo = sb("gu_lo", [P, 2, KC, 2 * IM], F32R)
        dn_hi = sb("dn_hi", [P, 2, NI, H], F32R)
        dn_lo = sb("dn_lo", [P, 2, NI, H], F32R)
        raw = sb("raw", [P, KC * 2 * IM])
        gu_raw = raw[:, :].rearrange("p (c i) -> p c i", c=KC)
        dn_raw = raw[:, 0:NI * H].rearrange("p (c n) -> p c n", c=NI)
        act_full = sb("act_full", [P, 2, L])
        act_hi = sb("act_hi", [P, RING, L], F32R)
        act_lo = sb("act_lo", [P, RING, L], F32R)

        expert_ids = sb("expert_ids", [P, E])
        tri = sb("tri", [P, P])
        ones = sb("ones", [P, P])
        tile_no = sb("tile_no", [P, TILES])
        tile_starts = sb("tile_starts", [P, N // TS])
        top_logit = sb("top_logit", [P, NT])
        probs = sb("router_probs", [P, NT, E])
        psum_ = sb("prob_sum", [P, NT])
        pinv = sb("prob_inv", [P, NT])
        top = sb("top", [P, NT, 8])
        top_at = sb("top_at", [P, NT, 8], U32)
        top_id = sb("top_id", [P, NT, TOPK])
        chosen = sb("chosen", [P, TOPK, NT, E])
        member = sb("member", [P, NT, E])
        ahead = sb("ahead", [P, NT + 1, E])
        over = probs[:, :, :].rearrange("p t e -> p (t e)")[:, 0:E * (N // TS)].rearrange("p (e n) -> p e n", e=E)
        tiles_of = sb("tiles_of", [P, E])
        start = sb("start", [P, E])
        zero_table = ahead[:, :, :].rearrange("p t e -> p (t e)")[:, 0:2 * CHUNKS].bitcast(I32)
        place = member
        at_k = probs
        slot_f = top_id
        slot_p, slot_c = (top_at[:, :, :].rearrange("p t k -> p (t k)")[:, half * NT * TOPK:(half + 1) * NT * TOPK]
                          for half in range(2))
        passed_by = chosen[:, :, :, :].rearrange("p k t e -> p (k t) e")[:, 0:TILES, :]
        expert_f = tile_no

        ps = ctx.enter_context(nc.psum_tensor("ps_shared", [P, 8, 512], F32))
        Y, COUNTS = 4, 7

        h_loaded = [sem(f"h_loaded{b}") for b in range(B)]
        w_loaded = sem("w_loaded")
        w_hi_ready = sem("w_hi_ready")
        w_lo_ready = sem("w_lo_ready")
        up_mm = sem("up_mm")
        silu_ready = sem("silu_ready")
        act_full_ready = sem("act_full_ready")
        act_hi_ready = sem("act_hi_ready")
        act_lo_ready = sem("act_lo_ready")
        down_mm = sem("down_mm")
        y_added = sem("y_added")
        consts_loaded = sem("route_consts_loaded")
        zeros_made = sem("zeros_made")
        zeros_stored = sem("zeros_stored")
        shifted_ready = sem("shifted_ready")
        route_exp = sem("route_exp")
        member_ready = sem("member_ready")
        count_mm = sem("count_mm")
        counts_taken = sem("counts_taken")
        places_ready = sem("places_ready")
        placed = sem("placed")
        step_done = sem("step_done")

        block = ctx.enter_context(nc.Block())

        @block.sync
        def _(sp):
            def load(s):
                sp.dma_start(raw[:, :], d["w_gu"][E + s]).then_inc(w_loaded, 16)
                if s == 0:
                    load_tokens(0)
                sp.wait_ge(w_lo_ready, s * PIECES + KC)
                sp.dma_start(raw[:, 0:NI * H], d["w_dn"][E + s]).then_inc(w_loaded, 16)

            def load_tokens(b):
                cols = slice(b * L, (b + 1) * L)
                for part, name in ((h_hi, "h2_hi"), (h_lo, "h2_lo")):
                    sp.dma_start(r32(part[:, :, cols]), r32(d[name][:, :, cols].rearrange("c p n -> p c n"))).then_inc(
                        h_loaded[b], 16)

            load(0)
            for out, name in ((expert_ids[:, :], "expert_ids"), (tri[:, :], "tri"), (tile_no[:, :], "tile_no"),
                              (tile_starts[:, :], "tile_starts"),
                              (t["pairs"][:, :, :, :].rearrange("p t k a -> p (t k a)"), "token_pairs")):
                sp.dma_start(out, d[name]).then_inc(consts_loaded, 16)
            for b in range(1, B):
                load_tokens(b)
            sp.wait_ge(zeros_made, 1)
            sp.dma_start(d["table"].rearrange("(p c) a -> p (c a)", p=P), zero_table).then_inc(zeros_stored, 16)
            for s in range(1, NS):
                sp.wait_ge(w_lo_ready, s * PIECES)
                load(s)

        @block.gpsimd
        def _(pool):
            def split_low(s, piece):
                pool.wait_ge(w_hi_ready, s * PIECES + piece + 1)
                raw, hi, lo = ((x[:, piece, :] for x in (gu_raw, gu_hi[:, s % 2, :, :], gu_lo[:, s % 2, :, :]))
                               if piece < KC else
                               (x[:, piece - KC, :] for x in (dn_raw, dn_hi[:, s % 2, :, :], dn_lo[:, s % 2, :, :])))
                nc.gpsimd.tensor_tensor(lo, raw, r32(hi), ALU.subtract).then_inc(w_lo_ready, 1)

            def put(n):
                i, k = n // TOPK, n % TOPK
                nc.gpsimd.indirect_dma_start(
                    d["table"], bass.IndirectOffsetOnAxis(ap=t["table_row"][:, i, k:k + 1], axis=0),
                    t["pairs"][:, i, k, :], None).then_inc(placed, 16)

            nc.gpsimd.memset(zero_table, 0).then_inc(zeros_made, 1)
            for piece in range(PIECES):
                split_low(0, piece)
            first_put = 4 * NI
            each = -(-NT * TOPK // (BLOCKS * NI - first_put))
            for m in range(BLOCKS * NI):
                rows = IC[m % NI][1]
                pool.wait_ge(act_hi_ready, m + 1)
                nc.gpsimd.tensor_tensor(act_lo[0:rows, m % RING, :], act_full[0:rows, m % 2, :],
                                        r32(act_hi[0:rows, m % RING, :]), ALU.subtract).then_inc(act_lo_ready, 1)
                s, piece = m // (B * NI), m % (B * NI) - NI
                if s + 1 < NS and 0 <= piece < PIECES:
                    split_low(s + 1, piece)
                if m == first_put:
                    pool.wait_ge(places_ready, 1)
                    pool.wait_ge(zeros_stored, 16)
                if m >= first_put:
                    for n in range((m - first_put) * each, min(NT * TOPK, (m - first_put + 1) * each)):
                        put(n)
            pool.wait_ge(placed, 16 * NT * TOPK)

        @block.scalar
        def _(act):
            nc.scalar.activation(t["shared_weight"][:, :], t["logits"][:, :, E], ACT.Exp, scale=-1.0).then_inc(
                route_exp, 1)
            act.wait_ge(shifted_ready, 1)
            nc.scalar.activation(probs[:, :, :], probs[:, :, :], ACT.Exp).then_inc(route_exp, 1)
            for m in range(BLOCKS * NI):
                rows = IC[m % NI][1]
                act.wait_ge(up_mm, m + 1)
                if m >= 2:
                    act.wait_ge(act_lo_ready, m - 1)
                nc.scalar.activation(act_full[0:rows, m % 2, :], ps[0:rows, 2 * (m % 2), :], ACT.Silu).then_inc(
                    silu_ready, 1)
                act.wait_ge(act_full_ready, m + 1)
                if m >= RING:
                    act.wait_ge(down_mm, ((m - RING) // NI + 1) * TT)
                nc.scalar.activation(act_hi[0:rows, m % RING, :], act_full[0:rows, m % 2, :], ACT.Copy).then_inc(
                    act_hi_ready, 1)

        @block.tensor
        def _(pe):
            def up(m):
                n, (at, rows) = m // NI, IC[m % NI]
                s, tb = n // B, n % B
                if s == 0 and m % NI == 0:
                    pe.wait_ge(h_loaded[tb], 32)
                if tb == 0 and m % NI == 0:
                    pe.wait_ge(w_lo_ready, s * PIECES + KC)
                if m >= 2:
                    pe.wait_ge(act_full_ready, m - 1)
                cols = slice(tb * L, (tb + 1) * L)
                for half in range(2):
                    w = slice(half * IM + at, half * IM + at + rows)
                    for c in range(KC):
                        last = three(nc, ps[0:rows, 2 * (m % 2) + half, :], gu_hi[:, s % 2, c, w],
                                     gu_lo[:, s % 2, c, w], h_hi[:, c, cols], h_lo[:, c, cols], c == 0, c == KC - 1)
                last.then_inc(up_mm, 1)

            def down(n):
                if n % B == 0:
                    pe.wait_ge(w_lo_ready, n // B * PIECES + PIECES)
                pe.wait_ge(act_lo_ready, (n + 1) * NI)
                for i in range(TT):
                    if n >= 1:
                        pe.wait_ge(y_added, (n - 1) * TT + i + 1)
                    if n == 1 and Y + i == COUNTS:
                        pe.wait_ge(counts_taken, 1)
                    q = slice(i * P, (i + 1) * P)
                    for c, (_, rows) in enumerate(IC):
                        m = n * NI + c
                        last = three(nc, ps[:, Y + i, :], act_hi[0:rows, m % RING, q], act_lo[0:rows, m % RING, q],
                                     dn_hi[0:rows, n // B % 2, c, :], dn_lo[0:rows, n // B % 2, c, :], c == 0,
                                     c == NI - 1)
                    last.then_inc(down_mm, 1)

            def count():
                pe.wait_ge(member_ready, 2)
                pe.wait_ge(y_added, TT)
                member_row = member[:, :, :].rearrange("p t e -> p (t e)")
                nc.tensor.matmul(ps[:, COUNTS, 0:NT * E], tri[:, :], member_row, start=True, stop=True)
                nc.tensor.matmul(ps[:, COUNTS, NT * E:2 * NT * E], ones[:, :], member_row, start=True,
                                 stop=True).then_inc(count_mm, 1)

            up(0)
            for n in range(BLOCKS):
                for m in range(n * NI + 1, min((n + 1) * NI + 1, BLOCKS * NI)):
                    up(m)
                if n == 1:
                    count()
                down(n)

        @block.vector
        def _(dve):
            done = [0]

            def step(ins):
                done[0] += 1
                ins.then_inc(step_done, 1)
                dve.wait_ge(step_done, done[0])

            def wide(ap, n=E):
                return ap.unsqueeze(2).to_broadcast([P, NT, n])

            def split_high(s, piece):
                if piece in (0, KC):
                    dve.wait_ge(w_loaded, s * 32 + (16 if piece == 0 else 32))
                if piece == 0 and s >= 2:
                    dve.wait_ge(down_mm, (s - 1) * B * TT)
                raw, hi = ((gu_raw[:, piece, :], gu_hi[:, s % 2, piece, :]) if piece < KC else
                           (dn_raw[:, piece - KC, :], dn_hi[:, s % 2, piece - KC, :]))
                nc.vector.tensor_copy(hi, raw).then_inc(w_hi_ready, 1)

            def shift_logits():
                logits = t["logits"][:, :, 0:E]
                step(nc.vector.tensor_reduce(top_logit[:, :], logits, AX.X, ALU.max))
                nc.vector.tensor_tensor(probs[:, :, :], logits, wide(top_logit[:, :]), ALU.subtract).then_inc(
                    shifted_ready, 1)

            def gate_and_softmax():
                dve.wait_ge(route_exp, 2)
                gate = t["shared_weight"]
                step(nc.vector.tensor_scalar_add(gate[:, :], gate[:, :], 1.0))
                step(nc.vector.reciprocal(gate[:, :], gate[:, :]))
                step(nc.vector.tensor_reduce(psum_[:, :], probs[:, :, :], AX.X, ALU.add))
                step(nc.vector.reciprocal(pinv[:, :], psum_[:, :]))
                step(nc.vector.tensor_tensor(probs[:, :, :], probs[:, :, :], wide(pinv[:, :]), ALU.mult))

            def top_four():
                for i in range(NT):
                    last = nc.vector.max(top[:, i, :], probs[:, i, :])
                step(last)
                for i in range(NT):
                    last = nc.vector.max_index(top_at[:, i, :], top[:, i, :], probs[:, i, :])
                step(last)
                step(nc.vector.tensor_copy(top_id[:, :, :], top_at[:, :, 0:TOPK]))

            def members():
                dve.wait_ge(consts_loaded, 16 * 5)
                ids = expert_ids[:, :].unsqueeze(1).to_broadcast([P, NT, E])
                for k in range(TOPK):
                    step(nc.vector.tensor_tensor(chosen[:, k, :, :], ids, top_id[:, :, k:k + 1].to_broadcast([P, NT, E]),
                                                 ALU.is_equal))
                step(nc.vector.tensor_tensor(member[:, :, :], chosen[:, 0, :, :], chosen[:, 1, :, :], ALU.add))
                step(nc.vector.tensor_tensor(member[:, :, :], member[:, :, :], chosen[:, 2, :, :], ALU.add))
                nc.vector.tensor_tensor(member[:, :, :], member[:, :, :], chosen[:, 3, :, :], ALU.add).then_inc(
                    member_ready, 1)
                nc.vector.memset(ones[:, :], 1.0).then_inc(member_ready, 1)

            def weights():
                step(nc.vector.tensor_reduce(psum_[:, :], top[:, :, 0:TOPK], AX.X, ALU.add))
                step(nc.vector.tensor_scalar_max(psum_[:, :], psum_[:, :], 1e-9))
                step(nc.vector.reciprocal(pinv[:, :], psum_[:, :]))
                step(nc.vector.tensor_tensor(t["pairs"][:, :, :, 1].bitcast(F32), top[:, :, 0:TOPK],
                                             wide(pinv[:, :], TOPK), ALU.mult))

            def take_counts():
                dve.wait_ge(count_mm, 1)
                dve.wait_ge(zeros_stored, 16)
                step(nc.vector.memset(ahead[:, 0, :], 0.0))
                for i in range(NT):
                    step(nc.vector.tensor_tensor(ahead[:, i + 1, :], ahead[:, i, :],
                                                 ps[:, COUNTS, (NT + i) * E:(NT + i + 1) * E], ALU.add))
                nc.vector.tensor_tensor(place[:, :, :], ahead[:, 0:NT, :],
                                        ps[:, COUNTS, 0:NT * E].rearrange("p (t e) -> p t e", e=E), ALU.add).then_inc(
                    counts_taken, 1)
                dve.wait_ge(counts_taken, 1)

            def tile_list():
                step(nc.vector.tensor_tensor(over[:, :, :], ahead[:, NT, :].unsqueeze(2).to_broadcast([P, E, N // TS]),
                                             tile_starts[:, :].unsqueeze(1).to_broadcast([P, E, N // TS]), ALU.is_gt))
                step(nc.vector.tensor_reduce(tiles_of[:, :], over[:, :, :], AX.X, ALU.add))
                step(nc.vector.memset(start[:, 0:1], 0.0))
                for e in range(1, E):
                    step(nc.vector.tensor_tensor(start[:, e:e + 1], start[:, e - 1:e], tiles_of[:, e - 1:e], ALU.add))

            def places():
                step(nc.vector.scalar_tensor_tensor(place[:, :, :], start[:, :].unsqueeze(1).to_broadcast([P, NT, E]),
                                                    float(TS), place[:, :, :], ALU.mult, ALU.add))
                for k in range(TOPK):
                    step(nc.vector.tensor_tensor(at_k[:, :, :], chosen[:, k, :, :], place[:, :, :], ALU.mult))
                    step(nc.vector.tensor_reduce(slot_f[:, :, k], at_k[:, :, :], AX.X, ALU.add))
                step(nc.vector.tensor_copy(t["slot"][:, :, :], slot_f[:, :, :]))
                slot_row = t["slot"][:, :, :].rearrange("p t k -> p (t k)")
                step(nc.vector.tensor_scalar(slot_c, slot_row, P.bit_length() - 1, None, ALU.logical_shift_right))
                step(nc.vector.tensor_scalar(slot_p, slot_row, P - 1, None, ALU.bitwise_and))
                nc.vector.scalar_tensor_tensor(t["table_row"][:, :, :].rearrange("p t k -> p (t k)"), slot_p,
                                               float(CHUNKS), slot_c, ALU.mult, ALU.add).then_inc(places_ready, 1)

            def tile_experts():
                step(nc.vector.tensor_tensor(tiles_of[:, :], tiles_of[:, :], start[:, :], ALU.add))
                step(nc.vector.tensor_tensor(passed_by, tiles_of[:, :].unsqueeze(1).to_broadcast([P, TILES, E]),
                                             tile_no[:, :].unsqueeze(2).to_broadcast([P, TILES, E]), ALU.is_le))
                step(nc.vector.tensor_reduce(expert_f[:, :], passed_by, AX.X, ALU.add))
                step(nc.vector.tensor_scalar_min(expert_f[:, :], expert_f[:, :], float(E - 1)))
                nc.vector.tensor_copy(t["tile_expert"][:, :], expert_f[:, :])

            def activate(m):
                rows = IC[m % NI][1]
                dve.wait_ge(silu_ready, m + 1)
                nc.vector.tensor_tensor(act_full[0:rows, m % 2, :], act_full[0:rows, m % 2, :],
                                        ps[0:rows, 2 * (m % 2) + 1, :], ALU.mult).then_inc(act_full_ready, 1)

            def add_outputs(n):
                for i in range(TT):
                    tile = n % B * TT + i
                    dve.wait_ge(down_mm, n * TT + i + 1)
                    weight = t["shared_weight"][:, tile:tile + 1]
                    if n < B:
                        nc.vector.tensor_scalar(acc[:, tile, :], ps[:, Y + i, :], weight, None, ALU.mult).then_inc(
                            y_added, 1)
                    else:
                        dve.wait_ge(y_added, (n - B) * TT + i + 1)
                        nc.vector.scalar_tensor_tensor(acc[:, tile, :], ps[:, Y + i, :], weight, acc[:, tile, :],
                                                       ALU.mult, ALU.add).then_inc(y_added, 1)

            shift_logits()
            for piece in range(PIECES):
                split_high(0, piece)
            gate_and_softmax()
            activate(0)
            top_four()
            for n in range(BLOCKS):
                for m in range(n * NI + 1, min((n + 1) * NI + 1, BLOCKS * NI)):
                    activate(m)
                    s, piece = (m - 1) // (B * NI), (m - 1) % (B * NI) - NI
                    if s + 1 < NS and 0 <= piece < PIECES:
                        split_high(s + 1, piece)
                    if m == 1:
                        members()
                    if m == 2:
                        weights()
                    if m == 2 * NI:
                        take_counts()
                    if m == 2 * NI + 1:
                        tile_list()
                    if m == 2 * NI + 2:
                        places()
                    if m == 3 * NI + 1:
                        tile_experts()
                add_outputs(n)


def routed_block(nc, t, d):
    with ExitStack() as ctx:
        def sb(name, shape, dt=F32):
            return ctx.enter_context(nc.sbuf_tensor(name, shape, dt))

        def sem(name):
            return ctx.enter_context(nc.semaphore(name))

        S = TS // P
        table = sb("table_in", [P, 2 * CHUNKS], I32)
        ident = sb("ident_moe", [P, P])
        index = sb("index", [P, 2, 2 * S], I32)
        weight = sb("slot_weight", [P, 2, 2 * S], I32)
        rows_in = sb("rows_in", [P, 2, S, H])
        h_hi = sb("h_tile_hi", [P, 2, KC, TS], F32R)
        h_lo = sb("h_tile_lo", [P, 2, KC, TS], F32R)
        gu_raw = sb("gu_raw2", [P, 2, KC, 2 * IM])
        dn_raw = sb("dn_raw2", [P, 2, NI, H])
        gu_hi = sb("gu_hi2", [P, 2, KC, 2 * IM], F32R)
        gu_lo = sb("gu_lo2", [P, 2, KC, 2 * IM], F32R)
        dn_hi = sb("dn_hi2", [P, 2, NI, H], F32R)
        dn_lo = sb("dn_lo2", [P, 2, NI, H], F32R)
        silu = sb("silu2", [P, 2, TS])
        act_full = sb("act_full2", [P, NI, TS])
        act_hi = sb("act_hi2", [P, NI + 1, TS], F32R)
        act_lo = sb("act_lo2", [P, NI + 1, TS], F32R)
        y = sb("y", [P, 2, S, H])
        ps = ctx.enter_context(nc.psum_tensor("ps_routed", [P, 8, 512], F32))
        T, U, Y = 0, 2, 5

        table_loaded = sem("table_loaded")
        gu_loaded = [sem(f"gu_loaded{par}") for par in range(2)]
        dn_loaded = [sem(f"dn_loaded{par}") for par in range(2)]
        gathered = [sem(f"gathered{par}") for par in range(2)]
        y_stored = [sem(f"y_stored{par}") for par in range(2)]
        index_ready = sem("index_ready")
        weight_ready = sem("weight_ready")
        gu_hi_ready = sem("gu_hi_ready")
        gu_lo_ready = sem("gu_lo_ready")
        dn_hi_ready = sem("dn_hi_ready")
        gu_lo_ready_v = sem("gu_lo_ready_v")
        dn_lo_ready = sem("dn_lo_ready")
        turned = sem("rows_turned")
        h_hi_ready = sem("h_tile_hi_ready")
        h_lo_ready = sem("h_tile_lo_ready")
        up_mm = sem("up_mm2")
        silu_ready = sem("silu_ready2")
        act_full_ready = sem("act_full_ready2")
        act_hi_ready = sem("act_hi_ready2")
        act_lo_ready = sem("act_lo_ready2")
        down_mm = sem("down_mm2")
        y_ready = sem("y_ready")
        passed = sem("passed2")

        SEED = 4
        seeded = (gu_lo_ready, gu_lo_ready_v, dn_lo_ready, turned, h_lo_ready, act_full_ready, act_lo_ready, down_mm,
                  y_ready, *y_stored)
        with nc.Block() as seeds:
            @seeds.gpsimd
            def _(pool):
                for semaphore in seeded:
                    pool.sem_inc(semaphore, SEED)

        def after(eng, semaphore, n):
            eng.wait_ge(semaphore, n + SEED)

        block = ctx.enter_context(nc.Block())

        def tiles(eng, body):
            with eng.Fori(0, TILES // 2 - 1) as pair:
                for par in range(2):
                    body(pair * 2 + par, par)
            for par in range(2):
                body(TILES - 2 + par, par, ending=True, last=(par == 1))

        def place(i, par):
            return NI if i == 0 and par == 1 else i

        def of_parity(j, par, each):
            return (j - par) * (each // 2) + each

        @block.sync
        def _(sp):
            sp.dma_start(table[:, :], d["table"].rearrange("(p c) a -> p (c a)", p=P)).then_inc(table_loaded, 16)
            sp.dma_start(ident[:, :], d["ident"]).then_inc(table_loaded, 16)
            with sp.Fori(0, TILES // 2) as pair:
                for par in range(2):
                    j = pair * 2 + par
                    e = bass.ds(sp.value_load(t["tile_expert"][0:1, bass.ds(j, 1)], min_val=0, max_val=E - 1), 1)
                    hold(sp, gu_lo_ready, j + (SEED - 1), passed)
                    hold(sp, gu_lo_ready_v, j * 2 + (SEED - 2), passed)
                    sp.dma_start(gu_raw[:, par, :, :].rearrange("p c i -> p (c i)"),
                                 d["w_gu"][e].rearrange("a p i -> (a p) i")).then_inc(gu_loaded[par], 16)
                    hold(sp, dn_lo_ready, j + (SEED - 1), passed)
                    sp.dma_start(dn_raw[:, par, :, :].rearrange("p c n -> p (c n)"),
                                 d["w_dn"][e].rearrange("a p n -> (a p) n")).then_inc(dn_loaded[par], 16)

        @block.gpsimd
        def _(pool):
            def gather(j, par, first=False):
                if not first:
                    hold(pool, turned, j + (SEED - 1), passed)
                nc.gpsimd.tensor_copy(index[:, par, :], table[:, bass.ds(j * 2 * S, 2 * S)]).then_inc(index_ready, 1)
                hold(pool, index_ready, j + 1, passed)
                for s in range(S):
                    nc.gpsimd.indirect_dma_start(
                        rows_in[:, par, s, :], None, d["h2_rows"],
                        bass.IndirectOffsetOnAxis(ap=index[:, par, 2 * s:2 * s + 1], axis=0)).then_inc(gathered[par], 16)

            def gu_low(j, par, c):
                pool.wait_ge(gu_hi_ready, j * KC + (c + 1))
                ins = nc.gpsimd.tensor_tensor(gu_lo[:, par, c, :], gu_raw[:, par, c, :], r32(gu_hi[:, par, c, :]),
                                              ALU.subtract)
                if c == 1:
                    ins.then_inc(gu_lo_ready, 1)

            def act_low(j, par, i):
                rows, at = IC[i][1], place(i, par)
                pool.wait_ge(act_hi_ready, j * NI + (i + 1))
                nc.gpsimd.tensor_tensor(act_lo[0:rows, at, :], act_full[0:rows, i, :], r32(act_hi[0:rows, at, :]),
                                        ALU.subtract).then_inc(act_lo_ready, 1)

            def body(j, par, ending=False, last=False):
                if not last:
                    gu_low(j + 1, 1 - par, 0)
                    gu_low(j + 1, 1 - par, 1)
                act_low(j, par, 1)
                if not ending:
                    gather(j + 2, par)
                act_low(j, par, 2)
                if not last:
                    act_low(j + 1, 1 - par, 0)

            pool.wait_ge(table_loaded, 32)
            gather(0, 0, first=True)
            gather(1, 1, first=True)
            for c in range(2):
                gu_low(0, 0, c)
            act_low(0, 0, 0)
            tiles(pool, body)

        @block.scalar
        def _(act):
            def h_high(j, par):
                for half in range(2):
                    after(act, turned, j + 1)
                    nc.scalar.activation(h_hi[:, par, 2 * half:2 * half + 2, :].rearrange("p c n -> p (c n)"),
                                         ps[:, T + half, :], ACT.Copy).then_inc(h_hi_ready, 1)

            def activate(j, par, i):
                rows = IC[i][1]
                act.wait_ge(up_mm, j * NI + (i + 1))
                nc.scalar.activation(silu[0:rows, i % 2, :], ps[0:rows, U + i, 0:TS], ACT.Silu).then_inc(
                    silu_ready, 1)
                after(act, act_full_ready, j * NI + (i + 1))
                nc.scalar.activation(act_hi[0:rows, place(i, par), :], act_full[0:rows, i, :], ACT.Copy).then_inc(
                    act_hi_ready, 1)

            def body(j, par, ending=False, last=False):
                activate(j, par, 1)
                if not last:
                    h_high(j + 1, 1 - par)
                activate(j, par, 2)
                if not last:
                    activate(j + 1, 1 - par, 0)
                    act.wait_ge(dn_loaded[1 - par], of_parity(j + 1, 1 - par, 16))
                    nc.scalar.activation(dn_hi[:, 1 - par, :, :], dn_raw[:, 1 - par, :, :], ACT.Copy).then_inc(
                        dn_hi_ready, 1)
                act.wait_ge(weight_ready, j + 1)
                for s in range(S):
                    after(act, down_mm, j * S + (s + 1))
                    if s == 0:
                        after(act, y_stored[par], (j - par) * 8)
                    nc.scalar.activation(y[:, par, s, :], ps[:, Y + s, :], ACT.Copy,
                                         scale=weight[:, par, 2 * s + 1:2 * s + 2].bitcast(F32)).then_inc(y_ready, 1)
                after(act, y_ready, j * S + S)
                act.dma_start(d["y"][bass.ds(j * TS, TS)].rearrange("(s p) n -> p s n", p=P),
                              y[:, par, :, :]).then_inc(y_stored[par], 16)

            h_high(0, 0)
            activate(0, 0, 0)
            tiles(act, body)
            for par in range(2):
                after(act, y_stored[par], TILES // 2 * 16)

        @block.tensor
        def _(pe):
            def turn(j, par):
                pe.wait_ge(gathered[par], of_parity(j, par, 16 * S))
                after(pe, h_lo_ready, (j - 1) * 2 + 2)
                for c in range(KC):
                    for s in range(S):
                        at = (c % 2) * TS + s * P
                        last = nc.tensor.transpose(ps[:, T + c // 2, at:at + P],
                                                   rows_in[:, par, s, c * P:(c + 1) * P], ident[:, :])
                last.then_inc(turned, 1)

            def up(j, par, i):
                at, rows = IC[i]
                if i == 0:
                    after(pe, gu_lo_ready, j + 1)
                    after(pe, gu_lo_ready_v, j * 2 + 2)
                    after(pe, h_lo_ready, j * 2 + 2)
                after(pe, act_full_ready, (j - 1) * NI + (i + 1))
                for half in range(2):
                    w = slice(half * IM + at, half * IM + at + rows)
                    for c in range(KC):
                        mm = three(nc, ps[0:rows, U + i, half * TS:(half + 1) * TS], gu_hi[:, par, c, w],
                                   gu_lo[:, par, c, w], h_hi[:, par, c, :], h_lo[:, par, c, :], c == 0, c == KC - 1)
                mm.then_inc(up_mm, 1)

            def body(j, par, ending=False, last=False):
                up(j, par, 1)
                if not last:
                    turn(j + 1, 1 - par)
                up(j, par, 2)
                if not last:
                    up(j + 1, 1 - par, 0)
                after(pe, dn_lo_ready, j + 1)
                after(pe, act_lo_ready, j * NI + NI)
                for s in range(S):
                    after(pe, y_ready, (j - 1) * S + (s + 1))
                    q = slice(s * P, (s + 1) * P)
                    for c, (_, rows) in enumerate(IC):
                        mm = three(nc, ps[:, Y + s, :], act_hi[0:rows, place(c, par), q],
                                   act_lo[0:rows, place(c, par), q], dn_hi[0:rows, par, c, :],
                                   dn_lo[0:rows, par, c, :], c == 0, c == NI - 1)
                    mm.then_inc(down_mm, 1)

            pe.wait_ge(table_loaded, 32)
            turn(0, 0)
            up(0, 0, 0)
            tiles(pe, body)

        @block.vector
        def _(dve):
            def gu_high(j, par, cs):
                for c in cs:
                    nc.vector.tensor_copy(gu_hi[:, par, c, :], gu_raw[:, par, c, :]).then_inc(gu_hi_ready, 1)

            def dn_high(j, par):
                nc.vector.tensor_copy(dn_hi[:, par, :, :], dn_raw[:, par, :, :]).then_inc(dn_hi_ready, 1)

            def dn_low(j, par):
                dve.wait_ge(dn_hi_ready, j + 1)
                nc.vector.tensor_tensor(dn_lo[:, par, :, :], dn_raw[:, par, :, :], r32(dn_hi[:, par, :, :]),
                                        ALU.subtract).then_inc(dn_lo_ready, 1)

            def gu_low(j, par, c):
                dve.wait_ge(gu_hi_ready, j * KC + (c + 1))
                nc.vector.tensor_tensor(gu_lo[:, par, c, :], gu_raw[:, par, c, :], r32(gu_hi[:, par, c, :]),
                                        ALU.subtract).then_inc(gu_lo_ready_v, 1)

            def h_low(j, par):
                for half in range(2):
                    dve.wait_ge(h_hi_ready, j * 2 + (half + 1))
                    out = (slice(None), par, slice(2 * half, 2 * half + 2))
                    nc.vector.tensor_tensor(h_lo[out].rearrange("p c n -> p (c n)"), ps[:, T + half, :],
                                            r32(h_hi[out].rearrange("p c n -> p (c n)")),
                                            ALU.subtract).then_inc(h_lo_ready, 1)

            def activate(j, i):
                rows = IC[i][1]
                dve.wait_ge(silu_ready, j * NI + (i + 1))
                after(dve, act_lo_ready, (j - 1) * NI + (i + 1))
                nc.vector.tensor_tensor(act_full[0:rows, i, :], silu[0:rows, i % 2, :], ps[0:rows, U + i, TS:2 * TS],
                                        ALU.mult).then_inc(act_full_ready, 1)

            def body(j, par, ending=False, last=False):
                column = bass.ds(j * 2 * S, 2 * S)
                if not last:
                    dve.wait_ge(gu_loaded[1 - par], of_parity(j + 1, 1 - par, 16))
                    gu_high(j + 1, 1 - par, range(KC))
                    gu_low(j + 1, 1 - par, 2)
                    gu_low(j + 1, 1 - par, 3)
                activate(j, 1)
                if not last:
                    h_low(j + 1, 1 - par)
                activate(j, 2)
                dn_low(j, par)
                nc.vector.tensor_copy(weight[:, par, :], table[:, column]).then_inc(weight_ready, 1)
                if not last:
                    activate(j + 1, 0)

            dve.wait_ge(table_loaded, 32)
            dve.wait_ge(gu_loaded[0], 16)
            gu_high(0, 0, range(KC))
            gu_low(0, 0, 2)
            gu_low(0, 0, 3)
            h_low(0, 0)
            dve.wait_ge(dn_loaded[0], 16)
            dn_high(0, 0)
            activate(0, 0)
            tiles(dve, body)


def combine_block(nc, t, d):
    with ExitStack() as ctx:
        def sb(name, shape, dt=F32):
            return ctx.enter_context(nc.sbuf_tensor(name, shape, dt))

        def sem(name):
            return ctx.enter_context(nc.semaphore(name))

        R = 4
        x1 = sb("x1_in", [P, B, TT, H])
        gb = sb("gb", [P, B, H])
        yk = sb("yk", [P, R, TOPK, H])
        loaded = [sem(f"x1_loaded{b}") for b in range(B)]
        y_in = [sem(f"y_in{r}") for r in range(R)]
        summed = sem("summed")
        stored = sem("out_stored")
        acc = t["acc"]
        block = ctx.enter_context(nc.Block())

        def tokens(ap, b):
            return ap[b].rearrange("(t p) n -> p t n", p=P)

        @block.sync
        def _(sp):
            def load(b):
                sp.dma_start(gb[:, b, :], d["mod_rows"][b:b + 1, 1, :].to_broadcast([P, H])).then_inc(loaded[b], 16)
                sp.dma_start(x1[:, b, :, :], tokens(d["x1"], b)).then_inc(loaded[b], 16)

            load(0)
            for i in range(NT):
                if i % TT == 1 and i // TT + 1 < B:
                    load(i // TT + 1)
                sp.wait_ge(summed, 5 * i + 5)
                sp.dma_start(tokens(d["out"], i // TT)[:, i % TT, :], x1[:, i // TT, i % TT, :]).then_inc(stored, 16)
            sp.wait_ge(stored, 16 * NT)

        @block.gpsimd
        def _(pool):
            for i in range(NT):
                if i >= R:
                    pool.wait_ge(summed, 5 * (i - R) + 3)
                for k in range(TOPK):
                    nc.gpsimd.indirect_dma_start(
                        yk[:, i % R, k, :], None, d["y"],
                        bass.IndirectOffsetOnAxis(ap=t["slot"][:, i, k:k + 1], axis=0)).then_inc(y_in[i % R], 16)

        @block.vector
        def _(dve):
            for i in range(NT):
                y = yk[:, i % R, :, :]
                if i % TT == 0:
                    dve.wait_ge(loaded[i // TT], 32)
                dve.wait_ge(y_in[i % R], 16 * TOPK * (i // R + 1))
                nc.vector.tensor_tensor(y[:, 0:2, :], y[:, 0:2, :], y[:, 2:4, :], ALU.add).then_inc(summed, 1)
                dve.wait_ge(summed, 5 * i + 1)
                nc.vector.tensor_tensor(acc[:, i, :], acc[:, i, :], y[:, 0, :], ALU.add).then_inc(summed, 1)
                dve.wait_ge(summed, 5 * i + 2)
                nc.vector.tensor_tensor(acc[:, i, :], acc[:, i, :], y[:, 1, :], ALU.add).then_inc(summed, 1)
                dve.wait_ge(summed, 5 * i + 3)
                nc.vector.tensor_tensor(acc[:, i, :], acc[:, i, :], gb[:, i // TT, :], ALU.mult).then_inc(summed, 1)
                dve.wait_ge(summed, 5 * i + 4)
                nc.vector.tensor_tensor(x1[:, i // TT, i % TT, :], x1[:, i // TT, i % TT, :], acc[:, i, :],
                                        ALU.add).then_inc(summed, 1)


def moe_block(nc, t, d):
    with ExitStack() as ctx:
        def sb(name, shape, dt=F32):
            t[name] = ctx.enter_context(nc.sbuf_tensor(name, shape, dt))

        sb("acc", [P, NT, H])
        sb("shared_weight", [P, NT])
        sb("slot", [P, NT, TOPK], U32)
        sb("table_row", [P, NT, TOPK], U32)
        sb("pairs", [P, NT, TOPK, 2], I32)
        sb("tile_expert", [P, TILES], I32)
        shared_block(nc, t, d)
        routed_block(nc, t, d)
        combine_block(nc, t, d)


SCRATCH = {
    "head_w": ((NH, P, SLOTS * P), F32R),
    "mod_rows": ((B, 4, H), F32),
    "x1": ((B, L, H), F32),
    "h2_rows": ((N, H), F32),
    "h2_hi": ((KC, P, N), F32R),
    "h2_lo": ((KC, P, N), F32R),
    "table": ((P * CHUNKS, 2), I32),
    "y": ((TILES * TS, H), F32),
}


_INPUTS = {
    "x": "L0_attn_x", "c": "L0_c", "wmod": "L0_wmod", "wq_down": "L0_attn_wq_down", "wq_up": "L0_attn_wq_up",
    "wq_rope": "L0_attn_wq_rope", "wkv_down": "L0_attn_wkv_down", "wk_up": "L0_attn_wk_up",
    "wv_up": "L0_attn_wv_up", "wk_rope": "L0_attn_wk_rope", "wo": "L0_attn_wo", "router_w": "L0_ffn_router_w",
    "sh_gate_w": "L0_ffn_sh_gate_w",
}


def expert_layout(inputs):
    import numpy as np
    part = {k: np.asarray(inputs[f"L0_ffn_{k}"]) for k in ("w_gate", "w_up", "w_down", "sh_gate", "sh_up", "sh_down")}
    gate, up = (np.concatenate([part[f"w_{k}"], part[f"sh_{k}"].reshape(H, NS, IM).transpose(1, 0, 2)])
                for k in ("gate", "up"))
    w_gu = np.concatenate([gate, up], axis=2).reshape(E + NS, KC, P, 2 * IM).transpose(0, 2, 1, 3)
    down = np.concatenate([part["w_down"], part["sh_down"].reshape(NS, IM, H)])
    w_dn = np.pad(down, ((0, 0), (0, NI * P - IM), (0, 0))).reshape(E + NS, NI, P, H).transpose(0, 2, 1, 3)
    return {"w_gu": np.ascontiguousarray(w_gu).reshape(E + NS, P, -1),
            "w_dn": np.ascontiguousarray(w_dn).reshape(E + NS, P, -1)}


def kernel(**inputs):
    import numpy as np
    import concourse.bacc as bacc
    from concourse.bass_utils import run_bass_kernel_spmd

    nc = bacc.Bacc("TRN2", target_bir_lowering=False, num_devices=1)
    arrays = {name: np.ascontiguousarray(inputs[key]) for name, key in _INPUTS.items()}
    arrays.update(expert_layout(inputs))
    arrays.update(shape_constants())
    d = {name: nc.dram_tensor(f"in_{name}", a.shape, mybir.dt.from_np(a.dtype), kind="ExternalInput").ap()
         for name, a in arrays.items()}
    for name, (shape, dt) in SCRATCH.items():
        d[name] = nc.dram_tensor(f"scratch_{name}", shape, dt).ap()
    d["out"] = nc.dram_tensor("out", (B, L, H), F32, kind="ExternalOutput").ap()
    block_kernel(nc, d)
    result = run_bass_kernel_spmd(nc, [{f"in_{name}": a for name, a in arrays.items()}], core_ids=[0])
    return result.results[0]["out"]
```
